# Optimizing a Trainium2 kernel written in Bass

```python
import numpy as np
import jax
import jax.numpy as jnp

def _softmax(x, axis=-1):
    return jax.nn.softmax(x, axis=axis)

def _gelu(x):
    return jax.nn.gelu(x, approximate=True)

def _silu(x):
    return jax.nn.silu(x)

def _sigmoid(x):
    return jax.nn.sigmoid(x)

def _layernorm(x, axis=-1, eps=1e-05):
    m = jnp.mean(x, axis=axis, keepdims=True)
    v = jnp.var(x, axis=axis, keepdims=True)
    return (x - m) / jnp.sqrt(v + eps)

def _scatter_add(tgt, idx, src, axis=0):
    return tgt.at[idx].add(src)

def _segment_sum(src, seg, n):
    return jax.ops.segment_sum(src, seg, n)
kernel_name = 'mk_perceiver_d1_seqx_r2_d25695'

def setup_inputs(seed: int=0):
    np.random.seed(seed)
    _w = jnp.asarray

    def _rec_inputs():
        import jax
        import jax.numpy as jnp
        _rk = jax.random.key(seed)
        x = -0.001547 + 1.001 * jax.random.normal(jax.random.fold_in(_rk, 1), (1, 512, 1024), jnp.float32)
        _lenS = 512 - jax.random.randint(jax.random.fold_in(_rk, 7), (1,), 0, max(1, 512 // 4) + 1, jnp.int32)
        _lenS2 = 8192 - jax.random.randint(jax.random.fold_in(_rk, 8), (1,), 0, max(1, 8192 // 4) + 1, jnp.int32)
        _ctx_2048P = jax.random.normal(jax.random.fold_in(_rk, 12), (1, 16, 1024), jnp.float32)
        _ctx_2048c = jax.random.dirichlet(jax.random.fold_in(_rk, 512), 0.3 * jnp.ones((16,), jnp.float32), (1, 8192))
        _ctx_2048t = jnp.einsum('bsk,bkd->bsd', _ctx_2048c, _ctx_2048P)
        _ctx_2048t = _ctx_2048t * jax.lax.rsqrt(jnp.mean(jnp.square(_ctx_2048t)) + 1e-12) * 0.953939
        ctx_2048 = -5.72187e-05 + 0.999849 * (_ctx_2048t + 0.3 * jax.random.normal(jax.random.fold_in(_rk, 612), (1, 8192, 1024), jnp.float32))
        _validS = jnp.arange(512)[None, :] < _lenS[:, None]
        _validS2 = jnp.arange(8192)[None, :] < _lenS2[:, None]
        _causal = jnp.tril(jnp.ones((512, 512), dtype=bool))
        mask_BxSxS2_ff0 = jnp.where(jnp.ones((1, 512, 8192), dtype=bool), 0.0, -1000000000.0).astype(jnp.float32)
        return (x, ctx_2048, mask_BxSxS2_ff0)
    x, ctx_2048, mask_BxSxS2_ff0 = _rec_inputs()

    def _L0_xattn_setup():
        import jax, jax.numpy as jnp
        import numpy as np
        B, Q_LEN, E = (8, 16, 1024)
        CACHE_LEN = 2048
        key = jax.random.key(seed)
        ks = jax.random.split(key, 9)
        s = 1.0 / np.sqrt(E)
        return {'x': jax.random.normal(ks[0], (B, Q_LEN, E), jnp.float32), 'attention_mask': jnp.zeros((B, Q_LEN, CACHE_LEN), jnp.float32), 'k_cache': jax.random.normal(ks[1], (B, CACHE_LEN, E), jnp.float32), 'v_cache': jax.random.normal(ks[2], (B, CACHE_LEN, E), jnp.float32), 'Wq': jax.random.normal(ks[3], (E, E), jnp.float32) * s, 'bq': jax.random.normal(ks[4], (E,), jnp.float32) * s, 'Wk': jax.random.normal(ks[5], (E, E), jnp.float32) * s, 'bk': jax.random.normal(ks[6], (E,), jnp.float32) * s, 'Wv': jax.random.normal(ks[7], (E, E), jnp.float32) * s, 'bv': jax.random.normal(ks[8], (E,), jnp.float32) * s}
    _L0_xattn_all = _L0_xattn_setup()
    _L0_xattn_in = {k: v for k, v in _L0_xattn_all.items() if k in ('Wq', 'bq', 'Wk', 'bk', 'Wv', 'bv')}
    del _L0_xattn_all

    def _L0_attn_setup():
        import jax, jax.numpy as jnp
        import numpy as np
        B, T, DIM = (2, 1024, 1024)
        H, HKV = (16, 4)
        HD = DIM // H
        KV_DIM = HKV * HD
        ROPE_DIMS = 64
        ROPE_BASE = 10000.0
        RANK = 16

        def _rope_cos_sin(seqlen, dtype):
            inv_freq = 1.0 / ROPE_BASE ** (jnp.arange(0, ROPE_DIMS, 2, dtype=jnp.float32) / ROPE_DIMS)
            freqs = jnp.arange(seqlen, dtype=jnp.float32)[:, None] * inv_freq[None, :]
            return (jnp.cos(freqs).astype(dtype), jnp.sin(freqs).astype(dtype))

        def _apply_rope(x, cos, sin):
            x_rope, x_pass = (x[..., :ROPE_DIMS], x[..., ROPE_DIMS:])
            half = ROPE_DIMS // 2
            x1, x2 = (x_rope[..., :half], x_rope[..., half:])
            rot = jnp.concatenate([x1 * cos + x2 * sin, -x1 * sin + x2 * cos], axis=-1)
            return jnp.concatenate([rot, x_pass], axis=-1)

        def _rms_norm(x):
            eps = jnp.finfo(x.dtype).eps
            return x * jax.lax.rsqrt(jnp.mean(x * x, axis=-1, keepdims=True) + eps)
        key = jax.random.key(seed)
        ks = jax.random.split(key, 15)
        n = lambda k, shape, scale: jax.random.normal(k, shape, jnp.float32) * scale
        d = {'x': n(ks[0], (B, T, DIM), 1.0), 'Wq': n(ks[1], (DIM, DIM), DIM ** (-0.5)), 'Wk': n(ks[2], (DIM, KV_DIM), DIM ** (-0.5)), 'Wv': n(ks[3], (DIM, KV_DIM), DIM ** (-0.5)), 'Wproj': n(ks[4], (DIM, DIM), DIM ** (-0.5)), 'q_gain': jnp.ones((H,), jnp.float32), 'q_A': n(ks[5], (DIM, RANK), DIM ** (-0.5)), 'q_B': n(ks[6], (RANK, DIM), 0.02), 'k_A': n(ks[7], (DIM, RANK), DIM ** (-0.5)), 'k_B': n(ks[8], (RANK, KV_DIM), 0.02), 'v_A': n(ks[9], (DIM, RANK), DIM ** (-0.5)), 'v_B': n(ks[10], (RANK, KV_DIM), 0.02), 'p_A': n(ks[11], (DIM, RANK), DIM ** (-0.5)), 'p_B': n(ks[12], (RANK, DIM), 0.02)}
        return d
    _L0_attn_all = _L0_attn_setup()
    _L0_attn_in = {k: v for k, v in _L0_attn_all.items() if k in ('Wq', 'Wk', 'Wv', 'Wproj', 'q_gain', 'q_A', 'q_B', 'k_A', 'k_B', 'v_A', 'v_B', 'p_A', 'p_B')}
    del _L0_attn_all

    def _L0_ffn_setup():
        import jax, jax.numpy as jnp
        import numpy as np
        HIDDEN = 1024
        MOE_INTER = 512
        SHARED_INTER = 2048
        N_EXPERTS = 16
        TOP_K = 2
        N_GROUP = 4
        TOPK_GROUP = 2
        NORM_TOPK_PROB = True
        ROUTED_SCALING = 1.0

        def relu2(x):
            r = jax.nn.relu(x)
            return r * r

        def _get_topk_indices(scores, e_bias):
            T, E = scores.shape
            s = scores + e_bias[None, :]
            gsz = E // N_GROUP
            group_scores = jax.lax.top_k(s.reshape(T, N_GROUP, gsz), 2)[0].sum(-1)
            group_idx = jax.lax.top_k(group_scores, TOPK_GROUP)[1]
            group_mask = jnp.zeros((T, N_GROUP), dtype=bool).at[jnp.arange(T)[:, None], group_idx].set(True)
            score_mask = jnp.repeat(group_mask, gsz, axis=1)
            masked = jnp.where(score_mask, s, 0.0)
            topk_indices = jax.lax.top_k(masked, TOP_K)[1]
            return jax.lax.stop_gradient(topk_indices)

        def _router(x_flat, router_weight, e_bias):
            logits = jnp.einsum('th,eh->te', x_flat.astype(jnp.float32), router_weight.astype(jnp.float32))
            scores = jax.nn.sigmoid(logits)
            topk_indices = _get_topk_indices(scores, e_bias)
            topk_weights = jnp.take_along_axis(scores, topk_indices, axis=1)
            if NORM_TOPK_PROB:
                topk_weights = topk_weights / (topk_weights.sum(-1, keepdims=True) + 1e-20)
            return (topk_indices, topk_weights * ROUTED_SCALING)
        key = jax.random.key(seed)
        ks = jax.random.split(key, 6)
        s = 0.02
        hidden_states = jax.random.normal(ks[0], (1, 1024, HIDDEN), dtype=jnp.float32)
        router_weight = jax.random.normal(ks[1], (N_EXPERTS, HIDDEN), dtype=jnp.float32) * s
        e_bias = jnp.zeros((N_EXPERTS,), dtype=jnp.float32)
        w_up = jax.random.normal(ks[2], (N_EXPERTS, HIDDEN, MOE_INTER), dtype=jnp.float32) * s
        w_down = jax.random.normal(ks[3], (N_EXPERTS, MOE_INTER, HIDDEN), dtype=jnp.float32) * s
        shared_up = jax.random.normal(ks[4], (HIDDEN, SHARED_INTER), dtype=jnp.float32) * s
        shared_down = jax.random.normal(ks[5], (SHARED_INTER, HIDDEN), dtype=jnp.float32) * s
        return {'hidden_states': hidden_states, 'router_weight': router_weight, 'e_bias': e_bias, 'w_up': w_up, 'w_down': w_down, 'shared_up': shared_up, 'shared_down': shared_down}
    _L0_ffn_all = _L0_ffn_setup()
    _L0_ffn_in = {k: v for k, v in _L0_ffn_all.items() if k in ('router_weight', 'e_bias', 'w_up', 'w_down', 'shared_up', 'shared_down')}
    del _L0_ffn_all
    return {'x': x, 'ctx_2048': ctx_2048, 'mask_BxSxS2_ff0': mask_BxSxS2_ff0, 'L0_xattn_Wq': _L0_xattn_in['Wq'], 'L0_xattn_bq': _L0_xattn_in['bq'], 'L0_xattn_Wk': _L0_xattn_in['Wk'], 'L0_xattn_bk': _L0_xattn_in['bk'], 'L0_xattn_Wv': _L0_xattn_in['Wv'], 'L0_xattn_bv': _L0_xattn_in['bv'], 'L0_attn_Wq': _L0_attn_in['Wq'], 'L0_attn_Wk': _L0_attn_in['Wk'], 'L0_attn_Wv': _L0_attn_in['Wv'], 'L0_attn_Wproj': _L0_attn_in['Wproj'], 'L0_attn_q_gain': _L0_attn_in['q_gain'], 'L0_attn_q_A': _L0_attn_in['q_A'], 'L0_attn_q_B': _L0_attn_in['q_B'], 'L0_attn_k_A': _L0_attn_in['k_A'], 'L0_attn_k_B': _L0_attn_in['k_B'], 'L0_attn_v_A': _L0_attn_in['v_A'], 'L0_attn_v_B': _L0_attn_in['v_B'], 'L0_attn_p_A': _L0_attn_in['p_A'], 'L0_attn_p_B': _L0_attn_in['p_B'], 'L0_ffn_router_weight': _L0_ffn_in['router_weight'], 'L0_ffn_e_bias': _L0_ffn_in['e_bias'], 'L0_ffn_w_up': _L0_ffn_in['w_up'], 'L0_ffn_w_down': _L0_ffn_in['w_down'], 'L0_ffn_shared_up': _L0_ffn_in['shared_up'], 'L0_ffn_shared_down': _L0_ffn_in['shared_down']}

def reference(x, ctx_2048, mask_BxSxS2_ff0, L0_xattn_Wq, L0_xattn_bq, L0_xattn_Wk, L0_xattn_bk, L0_xattn_Wv, L0_xattn_bv, L0_attn_Wq, L0_attn_Wk, L0_attn_Wv, L0_attn_Wproj, L0_attn_q_gain, L0_attn_q_A, L0_attn_q_B, L0_attn_k_A, L0_attn_k_B, L0_attn_v_A, L0_attn_v_B, L0_attn_p_A, L0_attn_p_B, L0_ffn_router_weight, L0_ffn_e_bias, L0_ffn_w_up, L0_ffn_w_down, L0_ffn_shared_up, L0_ffn_shared_down):
    import jax
    import jax.numpy as jnp

    def _L0_xattn_ref(x, attention_mask, k_cache, v_cache, Wq, bq, Wk, bk, Wv, bv):
        import jax, jax.numpy as jnp
        import numpy as np
        B, Q_LEN, E = (8, 16, 1024)
        CACHE_LEN = 2048
        Q = jnp.einsum('bqe,fe->bqf', x, Wq) + bq
        K_new = jnp.einsum('bqe,fe->bqf', x, Wk) + bk
        V_new = jnp.einsum('bqe,fe->bqf', x, Wv) + bv
        q_len = x.shape[1]
        end_step = attention_mask.shape[-1]
        past_kv_len = end_step - q_len
        k_cache = jax.lax.dynamic_update_slice(k_cache, K_new, (0, past_kv_len, 0))
        v_cache = jax.lax.dynamic_update_slice(v_cache, V_new, (0, past_kv_len, 0))
        K = k_cache[:, :end_step, :]
        V = v_cache[:, :end_step, :]
        scale = 1.0 / jnp.sqrt(jnp.asarray(Q.shape[-1], Q.dtype))
        scores = jnp.einsum('bqe,bke->bqk', Q, K) * scale + attention_mask
        attn = jax.nn.softmax(scores, axis=-1)
        return jnp.einsum('bqk,bke->bqe', attn, V)

    def _L0_attn_ref(x, Wq, Wk, Wv, Wproj, q_gain, q_A, q_B, k_A, k_B, v_A, v_B, p_A, p_B):
        import jax, jax.numpy as jnp
        import numpy as np
        B, T, DIM = (2, 1024, 1024)
        H, HKV = (16, 4)
        HD = DIM // H
        KV_DIM = HKV * HD
        ROPE_DIMS = 64
        ROPE_BASE = 10000.0
        RANK = 16

        def _rope_cos_sin(seqlen, dtype):
            inv_freq = 1.0 / ROPE_BASE ** (jnp.arange(0, ROPE_DIMS, 2, dtype=jnp.float32) / ROPE_DIMS)
            freqs = jnp.arange(seqlen, dtype=jnp.float32)[:, None] * inv_freq[None, :]
            return (jnp.cos(freqs).astype(dtype), jnp.sin(freqs).astype(dtype))

        def _apply_rope(x, cos, sin):
            x_rope, x_pass = (x[..., :ROPE_DIMS], x[..., ROPE_DIMS:])
            half = ROPE_DIMS // 2
            x1, x2 = (x_rope[..., :half], x_rope[..., half:])
            rot = jnp.concatenate([x1 * cos + x2 * sin, -x1 * sin + x2 * cos], axis=-1)
            return jnp.concatenate([rot, x_pass], axis=-1)

        def _rms_norm(x):
            eps = jnp.finfo(x.dtype).eps
            return x * jax.lax.rsqrt(jnp.mean(x * x, axis=-1, keepdims=True) + eps)
        bsz, seqlen, dim = x.shape
        group = H // HKV
        q = x @ Wq + x @ q_A @ q_B
        k = x @ Wk + x @ k_A @ k_B
        v = x @ Wv + x @ v_A @ v_B
        q = q.reshape(bsz, seqlen, H, HD).transpose(0, 2, 1, 3)
        k = k.reshape(bsz, seqlen, HKV, HD).transpose(0, 2, 1, 3)
        v = v.reshape(bsz, seqlen, HKV, HD).transpose(0, 2, 1, 3)
        q = _rms_norm(q)
        k = _rms_norm(k)
        cos, sin = _rope_cos_sin(seqlen, q.dtype)
        q = _apply_rope(q, cos, sin)
        k = _apply_rope(k, cos, sin)
        q = q * q_gain.astype(q.dtype)[None, :, None, None]
        qg = q.reshape(bsz, HKV, group, seqlen, HD)
        scale = HD ** (-0.5)
        scores = jnp.einsum('bkgtd,bksd->bkgts', qg, k) * scale
        causal = jnp.tril(jnp.ones((seqlen, seqlen), bool))
        scores = jnp.where(causal, scores, -jnp.inf)
        attn = jax.nn.softmax(scores, axis=-1)
        y = jnp.einsum('bkgts,bksd->bkgtd', attn, v)
        y_g = y.transpose(0, 3, 1, 2, 4)
        v_bt = v.transpose(0, 2, 1, 3)
        norm = jnp.sqrt(jnp.sum(v_bt * v_bt, axis=-1, keepdims=True))
        vn = (v_bt / jnp.maximum(norm, 1e-12))[:, :, :, None, :]
        proj = jnp.sum(y_g * vn, axis=-1, keepdims=True) * vn
        y_out = (y_g - proj).reshape(bsz, seqlen, dim)
        out = y_out @ Wproj + y_out @ p_A @ p_B
        return out

    def _L0_ffn_ref(hidden_states, router_weight, e_bias, w_up, w_down, shared_up, shared_down):
        import jax, jax.numpy as jnp
        import numpy as np
        HIDDEN = 1024
        MOE_INTER = 512
        SHARED_INTER = 2048
        N_EXPERTS = 16
        TOP_K = 2
        N_GROUP = 4
        TOPK_GROUP = 2
        NORM_TOPK_PROB = True
        ROUTED_SCALING = 1.0

        def relu2(x):
            r = jax.nn.relu(x)
            return r * r

        def _get_topk_indices(scores, e_bias):
            T, E = scores.shape
            s = scores + e_bias[None, :]
            gsz = E // N_GROUP
            group_scores = jax.lax.top_k(s.reshape(T, N_GROUP, gsz), 2)[0].sum(-1)
            group_idx = jax.lax.top_k(group_scores, TOPK_GROUP)[1]
            group_mask = jnp.zeros((T, N_GROUP), dtype=bool).at[jnp.arange(T)[:, None], group_idx].set(True)
            score_mask = jnp.repeat(group_mask, gsz, axis=1)
            masked = jnp.where(score_mask, s, 0.0)
            topk_indices = jax.lax.top_k(masked, TOP_K)[1]
            return jax.lax.stop_gradient(topk_indices)

        def _router(x_flat, router_weight, e_bias):
            logits = jnp.einsum('th,eh->te', x_flat.astype(jnp.float32), router_weight.astype(jnp.float32))
            scores = jax.nn.sigmoid(logits)
            topk_indices = _get_topk_indices(scores, e_bias)
            topk_weights = jnp.take_along_axis(scores, topk_indices, axis=1)
            if NORM_TOPK_PROB:
                topk_weights = topk_weights / (topk_weights.sum(-1, keepdims=True) + 1e-20)
            return (topk_indices, topk_weights * ROUTED_SCALING)
        orig_shape = hidden_states.shape
        x = hidden_states.reshape(-1, HIDDEN)
        T = x.shape[0]
        topk_indices, topk_weights = _router(x, router_weight, e_bias)
        combine = jnp.zeros((T, N_EXPERTS), dtype=topk_weights.dtype).at[jnp.arange(T)[:, None], topk_indices].add(topk_weights)
        h1 = jnp.einsum('th,ehi->tei', x, w_up)
        a = relu2(h1) * combine[:, :, None]
        routed = jnp.einsum('tei,eih->th', a, w_down)
        shared = relu2(hidden_states @ shared_up) @ shared_down
        return routed.reshape(orig_shape) + shared
    x = x + _L0_xattn_ref(_layernorm(x, axis=-1), mask_BxSxS2_ff0, ctx_2048, ctx_2048, L0_xattn_Wq, L0_xattn_bq, L0_xattn_Wk, L0_xattn_bk, L0_xattn_Wv, L0_xattn_bv)
    x = x + _L0_attn_ref(_layernorm(x, axis=-1), L0_attn_Wq, L0_attn_Wk, L0_attn_Wv, L0_attn_Wproj, L0_attn_q_gain, L0_attn_q_A, L0_attn_q_B, L0_attn_k_A, L0_attn_k_B, L0_attn_v_A, L0_attn_v_B, L0_attn_p_A, L0_attn_p_B)
    x = x + _L0_ffn_ref(_layernorm(x, axis=-1), L0_ffn_router_weight, L0_ffn_e_bias, L0_ffn_w_up, L0_ffn_w_down, L0_ffn_shared_up, L0_ffn_shared_down)
    return x

_drawn_inputs = setup_inputs


def setup_inputs(seed=0):
    import zlib

    import numpy as np

    out = dict(_drawn_inputs(seed))
    spreads = {'L0_attn_q_gain': (1.0, 0.6), 'L0_ffn_e_bias': (0.0, 0.663)}
    factors = {'L0_xattn_bq': 4.681,
     'L0_xattn_Wk': 5.479,
     'L0_xattn_bk': 64.0,
     'L0_xattn_Wv': 5.827,
     'L0_xattn_bv': 28.885,
     'L0_attn_q_A': 4.353,
     'L0_attn_q_B': 3.945,
     'L0_attn_k_A': 4.087,
     'L0_attn_k_B': 3.899,
     'ctx_2048': 8.0,
     'L0_attn_v_A': 8.0,
     'L0_attn_v_B': 8.0,
     'L0_attn_p_A': 8.0,
     'L0_attn_p_B': 8.0,
     'L0_ffn_router_weight': 6.866,
     'L0_ffn_w_up': 5.621,
     'L0_ffn_w_down': 5.21}
    for name, (base, spread) in spreads.items():
        noise = np.random.default_rng([zlib.crc32(name.encode()), seed]).standard_normal(out[name].shape)
        drawn = base * np.exp(spread * noise) if base else spread * noise
        out[name] = jnp.asarray(drawn.astype(out[name].dtype))
    for name, factor in factors.items():
        out[name] = (out[name] * factor).astype(out[name].dtype)
    return out
```

```python
from contextlib import ExitStack

import numpy as np

import concourse.bass as bass
from concourse import mybir

F32 = mybir.dt.float32
F32R = mybir.dt.float32r
I32 = mybir.dt.int32
ALU = mybir.AluOpType
ACT = mybir.ActivationFunctionType
AX = mybir.AxisListType

P = 128
T = 512
D = 1024
TB = T // P
DB = D // P
W = 512
LN_EPS = 1e-5


def f32(ap):
    return ap.bitcast(F32)


def matmul_3pass(out, lhs_hi, lhs_lo, rhs_hi, rhs_lo, first, last):
    def emit(pe):
        pe.matmul(out, lhs_hi, rhs_hi, start=first, stop=False)
        pe.matmul(out, lhs_hi, rhs_lo, start=False, stop=False)
        return pe.matmul(out, lhs_lo, rhs_hi, start=False, stop=last)
    return emit


class Memory:

    def __init__(self, nc, stack):
        self.nc, self.stack = nc, stack

    def sb(self, name, shape, dt=F32, stack=None):
        return (stack or self.stack).enter_context(self.nc.sbuf_tensor(name, shape, dt))

    def psum(self, name, shape, dt=F32, stack=None):
        return (stack or self.stack).enter_context(self.nc.psum_tensor(name, shape, dt))

    def sem(self, name):
        return self.stack.enter_context(self.nc.semaphore(name))


def make_identity(pool, ident, done):
    pool.memset(ident[:, :], 0.0).then_inc(done, 1)
    pool.wait_ge(done, 1)
    pool.affine_select(out=ident[:, :], in_=ident[:, :], compare_op=ALU.not_equal, fill=1.0,
                       base=0, pattern=[[-1, P]], channel_multiplier=1).then_inc(done, 1)


class LayerNorm:

    def __init__(self, m):
        self.bn_done = m.sem("ln_bn_done")
        self.aggr_done = m.sem("ln_aggr_done")
        self.eps_done = m.sem("ln_eps_done")
        self.rstd_done = m.sem("ln_rstd_done")
        self.xn_done = m.sem("ln_xn_done")

    def stats(self, dve, turn, x, stats, mean_var, tb):
        n = TB * turn + tb
        for h in range(2):
            dve.bn_stats(stats[:, tb, h, :], x[:, tb, h * W:(h + 1) * W]).then_inc(self.bn_done, 1)
        dve.wait_ge(self.bn_done, 2 * n + 2)
        dve.bn_aggr(mean_var[:, tb, :], stats[:, tb, :, :]).then_inc(self.aggr_done, 1)

    def rstd(self, pool, turn, mean_var, rstd, consts, tb):
        n = TB * turn + tb
        pool.wait_ge(self.aggr_done, n + 1)
        pool.tensor_tensor(rstd[:, tb:tb + 1], mean_var[:, tb, 1:2], consts[:, 0:1],
                           ALU.add).then_inc(self.eps_done, 1)
        pool.wait_ge(self.eps_done, n + 1)
        pool.tensor_tensor(rstd[:, tb:tb + 1], rstd[:, tb:tb + 1], consts[:, 1:2],
                           ALU.pow).then_inc(self.rstd_done, 1)

    def norm(self, dve, turn, x, xn, mean_var, rstd, tb):
        dve.wait_ge(self.rstd_done, TB * turn + tb + 1)
        dve.tensor_scalar(xn[:, tb, :], x[:, tb, :], mean_var[:, tb, 0:1],
                          rstd[:, tb:tb + 1], ALU.subtract, ALU.mult).then_inc(self.xn_done, 1)



def cross_projections(nc, m, ins, resid, QT, K, V, raw, kv_loaded, ident, ln):
    QT_hi, QT_lo = QT
    K_hi, K_lo = K
    V_hi, V_lo = V
    SCALE = 1.0 / float(np.sqrt(D))
    GROUPS = 6
    HALVES = 2 * GROUPS

    x_loaded = [m.sem(f"a_x_loaded{t}") for t in range(TB)]
    bias_loaded = m.sem("a_bias_loaded")
    w_loaded = [m.sem(f"a_w_loaded{h}") for h in range(2)]
    ident_done = m.sem("a_ident_done")
    consts_done = m.sem("a_consts_done")
    xt_ready, xt_hi_done, xt_lo_done = m.sem("a_xt_ready"), m.sem("a_xt_hi"), m.sem("a_xt_lo")
    w_hi_done, w_split, w_used = m.sem("a_w_hi"), m.sem("a_w_split"), m.sem("a_w_used")
    out_ready, biased, out_hi, out_lo = (m.sem("a_out_ready"), m.sem("a_biased"),
                                         m.sem("a_out_hi"), m.sem("a_out_lo"))

    with ExitStack() as stage:
        sb = lambda *a: m.sb(*a, stack=stage)
        stats = sb("a_stats", [P, TB, 2, 6])
        mean_var = sb("a_mean_var", [P, TB, 2])
        rstd = sb("a_rstd", [P, TB])
        consts = sb("a_consts", [P, 2])
        b_cols = sb("a_b_cols", [P, 2 * DB])
        bv_rows = sb("a_bv_rows", [P, D])
        tmp = sb("a_tmp", [P, 2, W])
        bank = m.psum("a_banks", [P, 8, W], stack=stage)
        xT_hi = V_hi[:, 1, :, :].rearrange("p b n -> p (b n)").rearrange("p (e t) -> p e t", t=T)
        xT_lo = V_lo[:, 1, :, :].rearrange("p b n -> p (b n)").rearrange("p (e t) -> p e t", t=T)

        def w_buf(t, w):
            return t[:, 1, 4 * (w % 2):4 * (w % 2) + 4, :]

        def out_tile(o, hi):
            g, i = divmod(o, 4)
            if g < 2:
                return (QT_hi if hi else QT_lo)[:, 4 * g + i, :]
            if g < 4:
                return (K_hi if hi else K_lo)[:, 0, 4 * (g - 2) + i, :]
            return (V_hi if hi else V_lo)[:, 0, i, (g - 4) * W:(g - 3) * W]

        with nc.Block() as block:
            @block.sync
            def _(sp):
                for t in range(TB):
                    sp.dma_start(resid[:, t, :], ins["x"][t]).then_inc(x_loaded[t], 16)
                for w in range(HALVES):
                    if w >= 2:
                        sp.wait_ge(w_split, w - 1)
                    sp.dma_start(raw[:, w % 2, :], ins["xattn_w"][w]).then_inc(w_loaded[w % 2], 16)
                for n in range(2):
                    sp.wait_ge(w_split, HALVES - 1 + n)
                    sp.dma_start(raw[:, n, :], ins["kv"][n]).then_inc(kv_loaded[n], 16)

            @block.gpsimd
            def _(pool):
                pool.dma_start(b_cols[:, :], ins["xattn_b_cols"]).then_inc(bias_loaded, 16)
                pool.dma_start(bv_rows[:, :], ins["xattn_bv"].to_broadcast([P, D])).then_inc(bias_loaded, 16)
                pool.memset(consts[:, 0:1], LN_EPS).then_inc(consts_done, 1)
                pool.memset(consts[:, 1:2], -0.5).then_inc(consts_done, 1)
                make_identity(pool, ident, ident_done)
                pool.wait_ge(consts_done, 2)
                for t in range(TB):
                    ln.rstd(pool, 0, mean_var, rstd, consts, t)

            @block.tensor
            def _(pe):
                pe.wait_ge(ident_done, 2)
                for n in range(2 * TB):
                    t, h = divmod(n, 2)
                    pe.wait_ge(ln.xn_done, t + 1)
                    if n >= 2:
                        pe.wait_ge(xt_lo_done, n - 1)
                    for i in range(4):
                        e = 4 * h + i
                        mm = pe.transpose(bank[:, 6 + n % 2, i * P:(i + 1) * P],
                                          resid[:, t, e * P:(e + 1) * P], ident[:, :])
                    mm.then_inc(xt_ready, 1)
                pe.wait_ge(xt_lo_done, 2 * TB)
                for w in range(HALVES):
                    g, h = divmod(w, 2)
                    pe.wait_ge(w_split, w + 1)
                    for i in range(4):
                        o = 4 * g + i
                        if h == 0 and g >= 2:
                            pe.wait_ge(biased, o - 7)
                        for j in range(4):
                            e = 4 * h + j
                            if g < 4:
                                lhs = [w_buf(x, w)[:, j, i * P:(i + 1) * P] for x in (K_hi, K_lo)]
                                rhs = [xT_hi[:, e, :], xT_lo[:, e, :]]
                            else:
                                lhs = [x[:, e, i * P:(i + 1) * P] for x in (xT_hi, xT_lo)]
                                rhs = [w_buf(x, w)[:, j, :] for x in (K_hi, K_lo)]
                            mm = matmul_3pass(bank[:, 4 * (g % 2) + i, :], *lhs, *rhs,
                                              first=e == 0, last=e == DB - 1)(pe)
                        if h == 1:
                            mm.then_inc(out_ready, 1)
                    if h == 0:
                        mm.then_inc(w_used, 1)

            @block.scalar
            def _(act):
                def weights_hi(w):
                    act.wait_ge(w_loaded[w % 2], 16 * (w // 2 + 1))
                    if w >= 2:
                        if w % 2 == 0:
                            act.wait_ge(w_used, w // 2)
                        else:
                            act.wait_ge(out_ready, 4 * (w // 2))
                    act.activation(w_buf(K_hi, w), raw[:, w % 2, :].rearrange("p (e n) -> p e n", n=W),
                                   ACT.Copy).then_inc(w_hi_done, 1)

                weights_hi(0)
                weights_hi(1)
                for n in range(2 * TB):
                    t, h = divmod(n, 2)
                    act.wait_ge(xt_ready, n + 1)
                    act.activation(xT_hi[:, 4 * h:4 * h + 4, t * P:(t + 1) * P],
                                   bank[:, 6 + n % 2, :].rearrange("p (e t) -> p e t", t=P),
                                   ACT.Copy).then_inc(xt_hi_done, 1)
                for g in range(GROUPS):
                    if 2 * g + 2 < HALVES:
                        weights_hi(2 * g + 2)
                    for o in range(4 * g, 4 * g + 4):
                        act.wait_ge(biased, o + 1)
                        act.activation(out_tile(o, True), tmp[:, o % 2, :], ACT.Copy).then_inc(out_hi, 1)
                    if 2 * g + 3 < HALVES:
                        weights_hi(2 * g + 3)

            @block.vector
            def _(dve):
                def weights_lo(w):
                    dve.wait_ge(w_hi_done, w + 1)
                    dve.tensor_tensor(w_buf(K_lo, w), raw[:, w % 2, :].rearrange("p (e n) -> p e n", n=W),
                                      f32(w_buf(K_hi, w)), ALU.subtract).then_inc(w_split, 1)

                for t in range(TB):
                    dve.wait_ge(x_loaded[t], 16)
                    ln.stats(dve, 0, resid, stats, mean_var, t)
                for t in range(TB):
                    ln.norm(dve, 0, resid, resid, mean_var, rstd, t)
                for n in range(2 * TB):
                    t, h = divmod(n, 2)
                    dve.wait_ge(xt_hi_done, n + 1)
                    dst = (slice(None), slice(4 * h, 4 * h + 4), slice(t * P, (t + 1) * P))
                    dve.tensor_tensor(xT_lo[dst], bank[:, 6 + n % 2, :].rearrange("p (e t) -> p e t", t=P),
                                      f32(xT_hi[dst]), ALU.subtract).then_inc(xt_lo_done, 1)
                weights_lo(0)
                weights_lo(1)
                dve.wait_ge(bias_loaded, 32)
                for g in range(GROUPS):
                    if 2 * g + 2 < HALVES:
                        weights_lo(2 * g + 2)
                    for o in range(4 * g, 4 * g + 4):
                        i = o % 4
                        dve.wait_ge(out_ready, o + 1)
                        if o >= 2:
                            dve.wait_ge(out_lo, o - 1)
                        psum = bank[:, 4 * (g % 2) + i, :]
                        if g < 2:
                            op = dve.tensor_scalar(tmp[:, o % 2, :], psum, b_cols[:, o:o + 1], SCALE,
                                                   ALU.add, ALU.mult)
                        elif g < 4:
                            op = dve.tensor_scalar(tmp[:, o % 2, :], psum, b_cols[:, o:o + 1], None, ALU.add)
                        else:
                            op = dve.tensor_tensor(tmp[:, o % 2, :], psum, bv_rows[:, (g - 4) * W:(g - 3) * W],
                                                   ALU.add)
                        op.then_inc(biased, 1)
                        dve.wait_ge(out_hi, o + 1)
                        dve.tensor_tensor(out_tile(o, False), tmp[:, o % 2, :], f32(out_tile(o, True)),
                                          ALU.subtract).then_inc(out_lo, 1)
                    if 2 * g + 3 < HALVES:
                        weights_lo(2 * g + 3)



def cross_attention(nc, m, ins, resid, QT, K, V, raw, kv_loaded, ident):
    QT_hi, QT_lo = QT
    K_hi, K_lo = K
    V_hi, V_lo = V
    CHUNKS = 16
    STEPS = TB * CHUNKS
    SPLITS = STEPS - TB
    BODY = 2 * TB

    mask_loaded = [m.sem(f"b_mask_loaded{i}") for i in range(4)]
    scores_ready = m.sem("b_scores_ready")
    masked = m.sem("b_masked")
    rowmax_done, newmax_done = m.sem("b_rowmax"), m.sem("b_newmax")
    stats_ready = m.sem("b_stats_ready")
    exp_done = m.sem("b_exp_done")
    pt_ready = m.sem("b_pt_ready")
    pt_hi_done, pt_lo_done = m.sem("b_pt_hi"), m.sem("b_pt_lo")
    pv_ready = m.sem("b_pv_ready")
    acc_done, sum_done = m.sem("b_acc_done"), m.sem("b_sum_done")
    kv_hi_done, kv_split = m.sem("b_kv_hi"), m.sem("b_kv_split")
    x_loaded, recip_done = m.sem("b_x_loaded"), m.sem("b_recip")

    with ExitStack() as stage:
        sb = lambda *a: m.sb(*a, stack=stage)
        s_sb = sb("b_scores", [P, 4, W])
        PT_hi = sb("b_PT_hi", [P, 2, W], F32R)
        PT_lo = sb("b_PT_lo", [P, 2, W], F32R)
        neg_rowmax = sb("b_neg_rowmax", [P, 2])
        neg_max = sb("b_neg_max", [P, 2, TB])
        change = sb("b_change", [P, TB])
        alpha = sb("b_alpha", [P, TB])
        rowsum = sb("b_rowsum", [P, TB])
        total = sb("b_total", [P, TB])
        S_ps = m.psum("b_S_ps", [P, 2, W], stack=stage)
        T_ps = m.psum("b_T_ps", [P, 2, W], stack=stage)
        O_ps = m.psum("b_O_ps", [P, 2, D], stack=stage)

        def split_tile(hi, u):
            par, q = (u // TB + 1) % 2, u % TB
            k, v = (K_hi, V_hi) if hi else (K_lo, V_lo)
            if q < 2:
                return k[:, par, 4 * q:4 * q + 4, :]
            return v[:, par, 2 * (q - 2):2 * (q - 2) + 2, :]

        def raw_tile(u):
            n = W if u % TB < 2 else D
            return raw[:, u % 2, :].rearrange("p (b n) -> p b n", n=n)

        def passes(engine, step, after):
            for u in range(BODY):
                step(0, u, u)
            with engine.Fori(1, STEPS // BODY - 1) as it:
                for u in range(BODY):
                    step(it * BODY, u, BODY)
            last = STEPS - BODY
            for u in range(BODY):
                step(last, u, last + u)
            after(STEPS)

        with nc.Block() as block:
            @block.sync
            def _(sp):
                def load(base, u):
                    sp.wait_ge(kv_split, base + (u - 1))
                    sp.dma_start(raw[:, u % 2, :], ins["kv"][base + u]).then_inc(kv_loaded[u % 2], 16)

                with sp.Fori(1, SPLITS // 2) as it:
                    for u in range(2):
                        load(it * 2, u)
                sp.wait_ge(kv_split, SPLITS)
                for t in range(TB):
                    sp.dma_start(raw[:, t // 2, (t % 2) * D:(t % 2 + 1) * D],
                                 ins["x"][t]).then_inc(x_loaded, 16)

            @block.gpsimd
            def _(pool):
                for u in range(4):
                    pool.dma_start(s_sb[:, u, :], ins["mask"][u]).then_inc(mask_loaded[u], 16)
                with pool.Fori(1, STEPS // 4) as it:
                    for u in range(4):
                        pool.wait_ge(pt_ready, it * 4 + (u - 3))
                        pool.dma_start(s_sb[:, u, :], ins["mask"][it * 4 + u]).then_inc(mask_loaded[u], 16)

            @block.tensor
            def _(pe):
                def scores(base, u, known):
                    par, qb = (u // TB) % 2, u % TB
                    if known >= TB and qb == 0:
                        pe.wait_ge(kv_split, base + (u - 2))
                    if known >= 2:
                        pe.wait_ge(masked, base + (u - 1))
                    for f in range(DB):
                        mm = matmul_3pass(S_ps[:, u % 2, :],
                                          QT_hi[:, f, qb * P:(qb + 1) * P], QT_lo[:, f, qb * P:(qb + 1) * P],
                                          K_hi[:, par, f, :], K_lo[:, par, f, :],
                                          first=f == 0, last=f == DB - 1)(pe)
                    mm.then_inc(scores_ready, 1)

                def transpose(base, u, known):
                    pe.wait_ge(exp_done, base + (u + 1))
                    if known >= 2:
                        pe.wait_ge(pt_lo_done, base + (u - 1))
                    for k in range(4):
                        mm = pe.transpose(T_ps[:, u % 2, k * P:(k + 1) * P],
                                          s_sb[:, u % 4, k * P:(k + 1) * P], ident[:, :])
                    mm.then_inc(pt_ready, 1)

                def values(base, u, known):
                    par, qb = (u // TB) % 2, u % TB
                    pe.wait_ge(pt_lo_done, base + (u + 1))
                    if known >= TB and qb == 0:
                        pe.wait_ge(kv_split, base + u)
                    if known >= 2:
                        pe.wait_ge(acc_done, base + (u - 1))
                    for k in range(4):
                        for h in range(2):
                            mm = matmul_3pass(O_ps[:, u % 2, h * W:(h + 1) * W],
                                              PT_hi[:, u % 2, k * P:(k + 1) * P],
                                              PT_lo[:, u % 2, k * P:(k + 1) * P],
                                              V_hi[:, par, k, h * W:(h + 1) * W],
                                              V_lo[:, par, k, h * W:(h + 1) * W],
                                              first=k == 0, last=k == 3)(pe)
                    mm.then_inc(pv_ready, 1)

                def step(base, u, known):
                    scores(base, u, known)
                    if known >= 1:
                        transpose(base, u - 1, known - 1)
                    if known >= 2:
                        values(base, u - 2, known - 2)

                def after(n):
                    transpose(0, n - 1, n - 1)
                    values(0, n - 2, n - 2)
                    values(0, n - 1, n - 1)

                passes(pe, step, after)

            @block.scalar
            def _(act):
                def pt_hi(base, u, known):
                    act.wait_ge(pt_ready, base + (u + 1))
                    if known >= 2:
                        act.wait_ge(pv_ready, base + (u - 1))
                    act.activation(PT_hi[:, u % 2, :], T_ps[:, u % 2, :], ACT.Copy).then_inc(pt_hi_done, 1)

                def step(base, u, known):
                    qb = u % TB
                    if known >= 1:
                        pt_hi(base, u - 1, known - 1)
                    act.wait_ge(stats_ready, base + (u + 1))
                    if known >= TB:
                        act.activation(alpha[:, qb:qb + 1], change[:, qb:qb + 1], ACT.Exp)
                    act.activation(s_sb[:, u % 4, :], s_sb[:, u % 4, :], ACT.Exp,
                                   bias=neg_max[:, (u // TB) % 2, qb:qb + 1],
                                   accum_out=rowsum[:, qb:qb + 1]).then_inc(exp_done, 1)
                    if known < SPLITS:
                        act.wait_ge(kv_loaded[u % 2], base * 8 + 16 * (u // 2 + 1))
                        if known >= TB:
                            act.wait_ge(scores_ready if qb < 2 else pv_ready, base + (u - qb))
                        act.activation(split_tile(True, u), raw_tile(u), ACT.Copy).then_inc(kv_hi_done, 1)

                passes(act, step, lambda n: pt_hi(0, n - 1, n - 1))

            @block.vector
            def _(dve):
                def pt_lo(base, u):
                    dve.wait_ge(pt_hi_done, base + (u + 1))
                    dve.tensor_tensor(PT_lo[:, u % 2, :], T_ps[:, u % 2, :], f32(PT_hi[:, u % 2, :]),
                                      ALU.subtract).then_inc(pt_lo_done, 1)

                def accumulate(base, u, known):
                    qb = u % TB
                    dve.wait_ge(pv_ready, base + (u + 1))
                    if known < TB:
                        op = dve.tensor_copy(resid[:, qb, :], O_ps[:, u % 2, :])
                    else:
                        op = dve.scalar_tensor_tensor(resid[:, qb, :], resid[:, qb, :], alpha[:, qb:qb + 1],
                                                      O_ps[:, u % 2, :], ALU.mult, ALU.add)
                    op.then_inc(acc_done, 1)

                def add_rowsum(base, u, known):
                    qb = u % TB
                    dve.wait_ge(exp_done, base + (u + 1))
                    if known < TB:
                        op = dve.tensor_copy(total[:, qb:qb + 1], rowsum[:, qb:qb + 1])
                    else:
                        dve.wait_ge(sum_done, base + (u - 3))
                        op = dve.scalar_tensor_tensor(total[:, qb:qb + 1], total[:, qb:qb + 1],
                                                      alpha[:, qb:qb + 1], rowsum[:, qb:qb + 1],
                                                      ALU.mult, ALU.add)
                    op.then_inc(sum_done, 1)

                def step(base, u, known):
                    par, qb = (u // TB) % 2, u % TB
                    now, before = neg_max[:, par, qb:qb + 1], neg_max[:, 1 - par, qb:qb + 1]
                    dve.wait_ge(scores_ready, base + (u + 1))
                    dve.wait_ge(mask_loaded[u % 4], base * 4 + 16 * (u // 4 + 1))
                    dve.tensor_tensor(s_sb[:, u % 4, :], S_ps[:, u % 2, :], s_sb[:, u % 4, :],
                                      ALU.add).then_inc(masked, 1)
                    dve.wait_ge(masked, base + (u + 1))
                    if known < TB:
                        dve.tensor_reduce(now, s_sb[:, u % 4, :], AX.X, ALU.max,
                                          negate=True).then_inc(stats_ready, 1)
                    else:
                        dve.tensor_reduce(neg_rowmax[:, u % 2:u % 2 + 1], s_sb[:, u % 4, :], AX.X, ALU.max,
                                          negate=True).then_inc(rowmax_done, 1)
                        dve.wait_ge(rowmax_done, base + (u + 1 - TB))
                        dve.tensor_tensor(now, before, neg_rowmax[:, u % 2:u % 2 + 1],
                                          ALU.min).then_inc(newmax_done, 1)
                        dve.wait_ge(newmax_done, base + (u + 1 - TB))
                        dve.tensor_tensor(change[:, qb:qb + 1], now, before,
                                          ALU.subtract).then_inc(stats_ready, 1)
                    if known >= 1:
                        add_rowsum(base, u - 1, known - 1)
                        pt_lo(base, u - 1)
                    if known < SPLITS:
                        dve.wait_ge(kv_hi_done, base + (u + 1))
                        dve.tensor_tensor(split_tile(False, u), raw_tile(u), f32(split_tile(True, u)),
                                          ALU.subtract).then_inc(kv_split, 1)
                    if known >= 2:
                        accumulate(base, u - 2, known - 2)

                def after(n):
                    add_rowsum(0, n - 1, n - 1)
                    pt_lo(0, n - 1)
                    accumulate(0, n - 2, n - 2)
                    accumulate(0, n - 1, n - 1)
                    dve.wait_ge(sum_done, n)
                    dve.reciprocal(total[:, :], total[:, :]).then_inc(recip_done, 1)
                    dve.wait_ge(recip_done, 1)
                    dve.wait_ge(acc_done, n)
                    dve.wait_ge(x_loaded, 16 * TB)
                    for t in range(TB):
                        dve.scalar_tensor_tensor(resid[:, t, :], resid[:, t, :], total[:, t:t + 1],
                                                 raw[:, t // 2, (t % 2) * D:(t % 2 + 1) * D],
                                                 ALU.mult, ALU.add).then_inc(recip_done, 1)

                passes(dve, step, after)




H, HKV, HD = 16, 4, 64
GROUP = H // HKV
RANK = 16
RMS_EPS = float(np.finfo(np.float32).eps)
MASKED = -1e30


def spread(ap, shape):
    return ap.to_broadcast(shape)


def self_attention(nc, m, ins, resid, ident, ln):
    QKV_HALVES, HALVES = 6, 10
    NB = 5
    PAIRS = H // 2
    UNITS = TB * PAIRS
    PIECES = 3 * TB

    names = """w_loaded0 w_loaded1 a_loaded0 a_loaded1 b_loaded tab_loaded consts_done causal_done
        xt_ready xt_hi_done xt_lo_done
        w_hi_done w_split w_used a_hi_done a_split b_hi_done b_split lr_ready lr_hi_done lr_lo_done
        out_ready piece_out ss_done ms_done rms_done gain_done gained normed cos_done sin_done
        rotated half_rotated qk_ready qk_read v_step vss vnorm vn_done
        s_ready s_masked s_max s_exp pt_ready pt_act pt_dve y_ready recip_done y_done
        yv dot along y_out""".split()
    s = {n: m.sem("c_" + n) for n in names}

    with ExitStack() as stage:
        sb = lambda *a: m.sb(*a, stack=stage)
        raw = sb("c_raw", [P, 2, 2048])
        w_hi, w_lo = sb("c_w_hi", [P, 2, 4, W], F32R), sb("c_w_lo", [P, 2, 4, W], F32R)
        xT_hi, xT_lo = sb("c_xT_hi", [P, DB, T], F32R), sb("c_xT_lo", [P, DB, T], F32R)
        xn = sb("c_xn", [P, TB, D])
        A_hi, A_lo = sb("c_A_hi", [P, DB, P], F32R), sb("c_A_lo", [P, DB, P], F32R)
        B_hi, B_lo = sb("c_B_hi", [P, NB, W], F32R), sb("c_B_lo", [P, NB, W], F32R)
        lr_hi, lr_lo = sb("c_lr_hi", [P, T], F32R), sb("c_lr_lo", [P, T], F32R)
        stats, mean_var = sb("c_stats", [P, TB, 2, 6]), sb("c_mean_var", [P, TB, 2])
        rstd, consts = sb("c_rstd", [P, TB]), sb("c_consts", [P, 3])
        cos, sin = sb("c_cos", [P, TB, HD // 2]), sb("c_sin", [P, TB, HD // 2])
        gain, causal = sb("c_gain", [P, H]), sb("c_causal", [P, P])
        v_sb, vn = sb("c_v", [P, TB, HKV * HD]), sb("c_vn", [P, TB, HKV * HD])
        vss = sb("c_vss", [P, TB * HKV])
        piece = sb("c_piece", [P, 2, W])
        sq = sb("c_sq", [P, 2, W])
        cosp = sb("c_cosp", [P, 2, W])
        ms = sb("c_ms", [P, 2, 8])
        qT = sb("c_qT", [P, PAIRS, T])
        kT = sb("c_kT", [P, HKV, T])
        p_sb, PT = sb("c_probs", [P, 2, 2, W]), sb("c_PT", [P, 2, 2, W])
        neg_max, rowsum, recip = sb("c_neg_max", [P, 2, 2]), sb("c_rowsum", [P, 2, 2]), sb("c_recip", [P, 4, 2])
        dots = sb("c_dots", [P, H])
        along = sb("c_along", [P, D])
        bank = m.psum("c_banks", [P, 8, W], stack=stage)
        a_raw = [x[:, :, :, :].rearrange("p a b n -> p (a b n)")[:, 0:D].rearrange("p (e n) -> p e n", n=P)
                 for x in (p_sb, PT)]
        b_raw = qT[:, 0:NB, :]

        def heads(j):
            return HKV if j < TB else 8

        def wide(t, j):
            return t[:, j % 2, 0:heads(j) * HD].rearrange("p (h d) -> p h d", d=HD)

        def half(t, j, k):
            return wide(t, j)[:, :, k * 32:(k + 1) * 32]

        def grouped(ap):
            return ap.rearrange("p (g a d) -> p g a d", g=HKV, d=HD)

        def vn_of(t):
            return vn[:, t, :].rearrange("p (g d) -> p g d", d=HD).unsqueeze(2)\
                .to_broadcast([P, HKV, GROUP, HD])

        def keys_of(u):
            return (u // PAIRS + 1) * P

        def rotated(j):
            if j < TB:
                return p_sb[:, j // 2, j % 2, :]
            return xn[:, j % TB, (j // TB - 1) * W:(j // TB) * W]

        def xt_bank(n, turn):
            return bank[:, (2 if turn else 6) + n % 2, :].rearrange("p (e t) -> p e t", t=P)

        def xt_tile(x, n):
            t, h = divmod(n, 2)
            return x[:, 4 * h:4 * h + 4, t * P:(t + 1) * P]

        with nc.Block() as block:
            @block.sync
            def _(sp):
                for w in range(HALVES):
                    if w >= 2:
                        sp.wait_ge(s["w_split"], w - 1)
                    sp.dma_start(raw[:, w % 2, :], ins["attn_w"][w]).then_inc(s[f"w_loaded{w % 2}"], 16)
                    if w == 0:
                        sp.dma_start(a_raw[0], ins["attn_A"][0]).then_inc(s["a_loaded0"], 16)
                    if w == 1:
                        sp.dma_start(b_raw, ins["attn_B"]).then_inc(s["b_loaded"], 16)
                        sp.dma_start(a_raw[1], ins["attn_A"][1]).then_inc(s["a_loaded1"], 16)

            @block.gpsimd
            def _(pool):
                pool.dma_start(cos[:, :, :], ins["cos"]).then_inc(s["tab_loaded"], 16)
                pool.dma_start(sin[:, :, :], ins["sin"]).then_inc(s["tab_loaded"], 16)
                pool.dma_start(gain[:, :], ins["gain"].to_broadcast([P, H])).then_inc(s["tab_loaded"], 16)
                for i, c in enumerate((LN_EPS, -0.5, 0.5)):
                    pool.memset(consts[:, i:i + 1], c).then_inc(s["consts_done"], 1)
                pool.memset(causal[:, :], 0.0).then_inc(s["causal_done"], 1)
                pool.wait_ge(s["causal_done"], 1)
                pool.affine_select(out=causal[:, :], in_=causal[:, :], compare_op=ALU.is_ge, fill=MASKED,
                                   base=0, pattern=[[-1, P]], channel_multiplier=1).then_inc(s["causal_done"], 1)
                pool.wait_ge(s["consts_done"], 3)
                for t in range(TB):
                    ln.rstd(pool, 1, mean_var, rstd, consts, t)
                pool.wait_ge(s["tab_loaded"], 48)
                for j in range(PIECES):
                    t, n = j % TB, heads(j)
                    pool.wait_ge(s["ss_done"], j + 1)
                    pool.tensor_scalar(ms[:, j % 2, 0:n], ms[:, j % 2, 0:n], 1.0 / HD, RMS_EPS,
                                       ALU.mult, ALU.add).then_inc(s["ms_done"], 1)
                    pool.wait_ge(s["ms_done"], j + 1)
                    pool.tensor_tensor(ms[:, j % 2, 0:n], ms[:, j % 2, 0:n],
                                       consts[:, 1:2].to_broadcast([P, n]), ALU.pow).then_inc(s["rms_done"], 1)
                    pool.wait_ge(s["normed"], j + 1)
                    for k in range(2):
                        pool.tensor_tensor(half(sq, j, k), half(piece, j, 1 - k),
                                           sin[:, t, :].unsqueeze(1).to_broadcast([P, n, 32]),
                                           ALU.mult).then_inc(s["sin_done"], 1)
                    if j == TB:
                        pool.wait_ge(s["vss"], 1)
                        pool.tensor_tensor(vss[:, :], vss[:, :], consts[:, 2:3].to_broadcast([P, TB * HKV]),
                                           ALU.pow).then_inc(s["vnorm"], 1)
                for t in range(TB):
                    pool.wait_ge(s["y_done"], PAIRS * (t + 1))
                    if t == 0:
                        pool.wait_ge(s["vn_done"], 1)
                    else:
                        pool.wait_ge(s["y_out"], t)
                    pool.tensor_tensor(grouped(along[:, :]), grouped(xn[:, t, :]), vn_of(t),
                                       ALU.mult).then_inc(s["yv"], 1)
                    pool.wait_ge(s["dot"], t + 1)
                    pool.tensor_tensor(grouped(along[:, :]), vn_of(t),
                                       dots[:, :].rearrange("p (g a) -> p g a", g=HKV).unsqueeze(3)
                                       .to_broadcast([P, HKV, GROUP, HD]), ALU.mult).then_inc(s["along"], 1)

            @block.tensor
            def _(pe):
                def turn_tokens(turn):
                    for n in range(2 * TB):
                        t, h = divmod(n, 2)
                        if turn:
                            pe.wait_ge(s["y_out"], t + 1)
                        else:
                            pe.wait_ge(ln.xn_done, TB + t + 1)
                        if n >= 2:
                            pe.wait_ge(s["xt_lo_done"], 2 * TB * turn + n - 1)
                        for i in range(4):
                            e = 4 * h + i
                            mm = pe.transpose(xt_bank(n, turn)[:, i, :], xn[:, t, e * P:(e + 1) * P], ident[:, :])
                        mm.then_inc(s["xt_ready"], 1)
                    pe.wait_ge(s["xt_lo_done"], 2 * TB * (turn + 1))

                def low_rank(turn):
                    pe.wait_ge(s["a_split"], turn + 1)
                    for e in range(DB):
                        mm = matmul_3pass(bank[:, 0 if turn else 4, :], A_hi[:, e, :], A_lo[:, e, :],
                                          xT_hi[:, e, :], xT_lo[:, e, :], e == 0, e == DB - 1)(pe)
                    mm.then_inc(s["lr_ready"], 1)

                def project(g):
                    for w in (2 * g, 2 * g + 1):
                        pe.wait_ge(s["w_split"], w + 1)
                        if w % 2:
                            pe.wait_ge(s["lr_lo_done"], 1 if w < QKV_HALVES else 2)
                        for t in range(TB):
                            out = bank[:, 4 * (g % 2) + t, :]
                            rows = slice(t * P, (t + 1) * P)
                            for j in range(4):
                                e = 4 * (w % 2) + j
                                mm = matmul_3pass(out, xT_hi[:, e, rows], xT_lo[:, e, rows],
                                                  w_hi[:, w % 2, j, :], w_lo[:, w % 2, j, :], e == 0, False)(pe)
                            if w % 2:
                                matmul_3pass(out, lr_hi[:, rows], lr_lo[:, rows], B_hi[:, g, :], B_lo[:, g, :],
                                             False, True)(pe).then_inc(s["out_ready"], 1)
                        if w % 2 == 0:
                            mm.then_inc(s["w_used"], 1)

                def turn_piece(j):
                    pe.wait_ge(s["rotated"], j + 1)
                    if j >= 4:
                        pe.wait_ge(s["qk_read"], j - 3)
                    for i in range(4):
                        mm = pe.transpose(bank[:, 4 + j % 4, i * P:(i + 1) * P],
                                          rotated(j)[:, i * P:(i + 1) * P], ident[:, :])
                    mm.then_inc(s["qk_ready"], 1)

                def scores(u):
                    qb, p = divmod(u, PAIRS)
                    n = keys_of(u)
                    if u >= 2:
                        pe.wait_ge(s["s_exp"], u - 1)
                    for h in range(2):
                        rows = slice(HD * h, HD * h + HD)
                        mm = pe.matmul(bank[:, 2 * (u % 2) + h, 0:n], qT[rows, p, qb * P:(qb + 1) * P],
                                       kT[rows, 2 * p // GROUP, 0:n], start=True, stop=True)
                    mm.then_inc(s["s_ready"], 1)

                def transpose(u):
                    pe.wait_ge(s["s_exp"], u + 1)
                    if u >= 1:
                        pe.wait_ge(s["pt_act"], u)
                        pe.wait_ge(s["pt_dve"], u)
                    for h in range(2):
                        for k in range(keys_of(u) // P):
                            mm = pe.transpose(bank[:, 4 + h, k * P:(k + 1) * P],
                                              p_sb[:, u % 2, h, k * P:(k + 1) * P], ident[:, :])
                    mm.then_inc(s["pt_ready"], 1)

                def values(u):
                    g = 2 * (u % PAIRS) // GROUP
                    pe.wait_ge(s["pt_act"], u + 1)
                    pe.wait_ge(s["pt_dve"], u + 1)
                    if u >= 2:
                        pe.wait_ge(s["y_done"], u - 1)
                    blocks = keys_of(u) // P
                    for h in range(2):
                        for k in range(blocks):
                            mm = pe.matmul(bank[:, 6 + u % 2, h * HD:(h + 1) * HD],
                                           PT[:, u % 2, h, k * P:(k + 1) * P], v_sb[:, k, g * HD:(g + 1) * HD],
                                           start=k == 0, stop=k == blocks - 1)
                    mm.then_inc(s["y_ready"], 1)

                turn_tokens(0)
                low_rank(0)
                pe.wait_ge(s["b_split"], 1)
                project(0)
                project(1)
                pe.wait_ge(s["piece_out"], TB)
                project(2)
                pe.wait_ge(s["piece_out"], 2 * TB)
                for j in range(PIECES):
                    turn_piece(j)
                pe.wait_ge(s["qk_read"], PIECES)
                pe.wait_ge(s["piece_out"], PIECES)
                for u in range(UNITS + 2):
                    if u < UNITS:
                        scores(u)
                    if 1 <= u <= UNITS:
                        transpose(u - 1)
                    if u >= 2:
                        values(u - 2)
                turn_tokens(1)
                low_rank(1)
                project(3)
                project(4)

            @block.scalar
            def _(act):
                def weights_hi(w):
                    act.wait_ge(s[f"w_loaded{w % 2}"], 16 * (w // 2 + 1))
                    if w >= 2:
                        if w % 2 == 0:
                            act.wait_ge(s["w_used"], w // 2)
                        else:
                            act.wait_ge(s["out_ready"], 4 * (w // 2))
                    act.activation(w_hi[:, w % 2, :, :], raw[:, w % 2, :].rearrange("p (e n) -> p e n", n=W),
                                   ACT.Copy).then_inc(s["w_hi_done"], 1)

                def xt_hi(turn):
                    for n in range(2 * TB):
                        act.wait_ge(s["xt_ready"], 2 * TB * turn + n + 1)
                        act.activation(xt_tile(xT_hi, n), xt_bank(n, turn), ACT.Copy).then_inc(s["xt_hi_done"], 1)

                def a_hi(turn):
                    act.wait_ge(s[f"a_loaded{turn}"], 16)
                    if turn:
                        act.wait_ge(s["lr_ready"], 1)
                    act.activation(A_hi[:, :, :], a_raw[turn], ACT.Copy).then_inc(s["a_hi_done"], 1)

                def low_rank_hi(turn):
                    act.wait_ge(s["lr_ready"], turn + 1)
                    act.activation(lr_hi[:, :], bank[:, 0 if turn else 4, :], ACT.Copy).then_inc(s["lr_hi_done"], 1)

                def take_piece(j):
                    n = heads(j) * HD
                    psum = bank[:, 4 * ((j // TB) % 2) + j % TB, :]
                    act.wait_ge(s["out_ready"], j + 1)
                    if j >= 2:
                        act.wait_ge(s["rotated"], j - 1)
                    act.activation(piece[:, j % 2, 0:n], psum[:, 0:n], ACT.Copy)
                    if j < TB:
                        act.activation(v_sb[:, j, :], psum[:, n:2 * n], ACT.Copy)
                    act.activation(sq[:, j % 2, 0:n], psum[:, 0:n], ACT.Square).then_inc(s["piece_out"], 1)

                def turned_piece(j):
                    act.wait_ge(s["qk_ready"], j + 1)
                    t = j % TB
                    dst = kT[:, :, t * P:(t + 1) * P] if j < TB else \
                        qT[:, 4 * (j // TB - 1):4 * (j // TB), t * P:(t + 1) * P]
                    act.activation(dst, bank[:, 4 + j % 4, :].rearrange("p (e t) -> p e t", t=P),
                                   ACT.Copy).then_inc(s["qk_read"], 1)

                def pt_act(u):
                    n = keys_of(u)
                    act.wait_ge(s["pt_ready"], u + 1)
                    if u >= 2:
                        act.wait_ge(s["y_ready"], u - 1)
                    act.activation(PT[:, u % 2, 0, 0:n], bank[:, 4, 0:n], ACT.Copy).then_inc(s["pt_act"], 1)

                def exps(u):
                    n = keys_of(u)
                    act.wait_ge(s["s_max"], u + 1)
                    if u >= 2:
                        act.wait_ge(s["pt_ready"], u - 1)
                        act.wait_ge(s["recip_done"], u - 1)
                    for h in range(2):
                        op = act.activation(p_sb[:, u % 2, h, 0:n], bank[:, 2 * (u % 2) + h, 0:n], ACT.Exp,
                                            bias=neg_max[:, u % 2, h:h + 1], accum_out=rowsum[:, u % 2, h:h + 1])
                    op.then_inc(s["s_exp"], 1)

                weights_hi(0)
                weights_hi(1)
                a_hi(0)
                act.wait_ge(s["b_loaded"], 16)
                act.activation(B_hi[:, :, :], b_raw, ACT.Copy).then_inc(s["b_hi_done"], 1)
                xt_hi(0)
                low_rank_hi(0)
                weights_hi(2)
                for g in range(3):
                    take_piece(4 * g)
                    take_piece(4 * g + 1)
                    weights_hi(2 * g + 3)
                    take_piece(4 * g + 2)
                    take_piece(4 * g + 3)
                    if g < 2:
                        weights_hi(2 * g + 4)
                a_hi(1)
                for j in range(PIECES):
                    turned_piece(j)
                for u in range(UNITS):
                    if u >= 1:
                        pt_act(u - 1)
                    exps(u)
                pt_act(UNITS - 1)
                xt_hi(1)
                low_rank_hi(1)
                weights_hi(8)
                weights_hi(9)

            @block.vector
            def _(dve):
                def weights_lo(w):
                    dve.wait_ge(s["w_hi_done"], w + 1)
                    dve.tensor_tensor(w_lo[:, w % 2, :, :], raw[:, w % 2, :].rearrange("p (e n) -> p e n", n=W),
                                      f32(w_hi[:, w % 2, :, :]), ALU.subtract).then_inc(s["w_split"], 1)

                def xt_lo(turn):
                    for n in range(2 * TB):
                        dve.wait_ge(s["xt_hi_done"], 2 * TB * turn + n + 1)
                        dve.tensor_tensor(xt_tile(xT_lo, n), xt_bank(n, turn), f32(xt_tile(xT_hi, n)),
                                          ALU.subtract).then_inc(s["xt_lo_done"], 1)

                def a_lo(turn):
                    dve.wait_ge(s["a_hi_done"], turn + 1)
                    dve.tensor_tensor(A_lo[:, :, :], a_raw[turn], f32(A_hi[:, :, :]),
                                      ALU.subtract).then_inc(s["a_split"], 1)

                def low_rank_lo(turn):
                    dve.wait_ge(s["lr_hi_done"], turn + 1)
                    dve.tensor_tensor(lr_lo[:, :], bank[:, 0 if turn else 4, :], f32(lr_hi[:, :]),
                                      ALU.subtract).then_inc(s["lr_lo_done"], 1)

                def rotate_piece(j):
                    t, n = j % TB, heads(j)
                    scale = ms[:, j % 2, 0:n]
                    dve.wait_ge(s["piece_out"], j + 1)
                    dve.tensor_reduce(scale, wide(sq, j), AX.X, ALU.add).then_inc(s["ss_done"], 1)
                    dve.wait_ge(s["rms_done"], j + 1)
                    if j >= TB:
                        first = 8 * (j // TB - 1)
                        dve.tensor_tensor(scale, scale, gain[:, first:first + 8], ALU.mult).then_inc(s["gained"], 1)
                        dve.wait_ge(s["gained"], j - TB + 1)
                    dve.tensor_tensor(wide(piece, j), wide(piece, j), scale.unsqueeze(2).to_broadcast([P, n, HD]),
                                      ALU.mult).then_inc(s["normed"], 1)
                    dve.wait_ge(s["normed"], j + 1)
                    dve.tensor_tensor(wide(cosp, j).rearrange("p h (k d) -> p h k d", k=2),
                                      wide(piece, j).rearrange("p h (k d) -> p h k d", k=2),
                                      cos[:, t, :].unsqueeze(1).unsqueeze(1).to_broadcast([P, n, 2, 32]),
                                      ALU.mult).then_inc(s["cos_done"], 1)
                    dve.wait_ge(s["cos_done"], j + 1)
                    dve.wait_ge(s["sin_done"], 2 * j + 2)
                    for k, op in enumerate((ALU.add, ALU.subtract)):
                        if j < TB:
                            out = rotated(j).rearrange("p (h c d) -> p h c d", h=n, c=2)[:, :, :, k * 32:(k + 1) * 32]
                            in0, in1 = (half(x, j, k).unsqueeze(2).to_broadcast([P, n, 2, 32]) for x in (cosp, sq))
                        else:
                            out = rotated(j).rearrange("p (h d) -> p h d", d=HD)[:, :, k * 32:(k + 1) * 32]
                            in0, in1 = half(cosp, j, k), half(sq, j, k)
                        ins_ = dve.tensor_tensor(out, in0, in1, op)
                    ins_.then_inc(s["rotated"], 1)

                def unit_values():
                    v3 = lambda x: x.rearrange("p (h d) -> p h d", d=HD)
                    v_flat = v_sb[:, :, :].rearrange("p t n -> p (t n)")
                    dve.tensor_tensor(along[:, :], v_flat, v_flat, ALU.mult).then_inc(s["v_step"], 1)
                    dve.wait_ge(s["v_step"], 1)
                    dve.tensor_reduce(vss[:, :], v3(along[:, :]), AX.X, ALU.add).then_inc(s["vss"], 1)

                def unit_values_2():
                    v3 = lambda x: x.rearrange("p (h d) -> p h d", d=HD)
                    dve.wait_ge(s["vnorm"], 1)
                    dve.tensor_scalar(vss[:, :], vss[:, :], 1e-12, None, ALU.max).then_inc(s["v_step"], 1)
                    dve.wait_ge(s["v_step"], 2)
                    dve.reciprocal(vss[:, :], vss[:, :]).then_inc(s["v_step"], 1)
                    dve.wait_ge(s["v_step"], 3)
                    dve.tensor_tensor(v3(vn[:, :, :].rearrange("p t n -> p (t n)")),
                                      v3(v_sb[:, :, :].rearrange("p t n -> p (t n)")),
                                      vss[:, :].unsqueeze(2).to_broadcast([P, TB * HKV, HD]),
                                      ALU.mult).then_inc(s["vn_done"], 1)

                def maxima(u):
                    n = keys_of(u)
                    dve.wait_ge(s["s_ready"], u + 1)
                    pair = bank[:, 2 * (u % 2):2 * (u % 2) + 2, :]
                    dve.tensor_tensor(pair[:, :, n - P:n], pair[:, :, n - P:n],
                                      causal[:, :].unsqueeze(1).to_broadcast([P, 2, P]),
                                      ALU.add).then_inc(s["s_masked"], 1)
                    dve.wait_ge(s["s_masked"], u + 1)
                    dve.tensor_reduce(neg_max[:, u % 2, :], pair[:, :, 0:n], AX.X, ALU.max,
                                      negate=True).then_inc(s["s_max"], 1)

                def pt_dve(u):
                    n = keys_of(u)
                    dve.wait_ge(s["pt_ready"], u + 1)
                    if u >= 2:
                        dve.wait_ge(s["y_ready"], u - 1)
                    dve.tensor_copy(PT[:, u % 2, 1, 0:n], bank[:, 5, 0:n]).then_inc(s["pt_dve"], 1)

                def row_recip(u):
                    dve.wait_ge(s["s_exp"], u + 1)
                    dve.reciprocal(recip[:, u % 4, :], rowsum[:, u % 2, :]).then_inc(s["recip_done"], 1)

                def take_y(u):
                    qb, p = divmod(u, PAIRS)
                    dve.wait_ge(s["y_ready"], u + 1)
                    dve.wait_ge(s["recip_done"], u + 1)
                    dve.tensor_tensor(xn[:, qb, p * P:(p + 1) * P].rearrange("p (h d) -> p h d", d=HD),
                                      bank[:, 6 + u % 2, 0:P].rearrange("p (h d) -> p h d", d=HD),
                                      recip[:, u % 4, :].unsqueeze(2).to_broadcast([P, 2, HD]),
                                      ALU.mult).then_inc(s["y_done"], 1)

                def dot(t):
                    dve.wait_ge(s["yv"], t + 1)
                    dve.tensor_reduce(dots[:, :], along[:, :].rearrange("p (h d) -> p h d", d=HD),
                                      AX.X, ALU.add).then_inc(s["dot"], 1)

                def take_along(t):
                    dve.wait_ge(s["along"], t + 1)
                    dve.tensor_tensor(xn[:, t, :], xn[:, t, :], along[:, :], ALU.subtract).then_inc(s["y_out"], 1)

                for t in range(TB):
                    ln.stats(dve, 1, resid, stats, mean_var, t)
                for t in range(TB):
                    ln.norm(dve, 1, resid, xn, mean_var, rstd, t)
                weights_lo(0)
                weights_lo(1)
                a_lo(0)
                dve.wait_ge(s["b_hi_done"], 1)
                dve.tensor_tensor(B_lo[:, :, :], b_raw, f32(B_hi[:, :, :]),
                                  ALU.subtract).then_inc(s["b_split"], 1)
                xt_lo(0)
                low_rank_lo(0)
                dve.wait_ge(s["tab_loaded"], 48)
                dve.tensor_scalar(gain[:, :], gain[:, :], float(HD) ** -0.5, None, ALU.mult).then_inc(s["gain_done"], 1)
                dve.wait_ge(s["gain_done"], 1)
                weights_lo(2)
                for g in range(3):
                    rotate_piece(4 * g)
                    rotate_piece(4 * g + 1)
                    weights_lo(2 * g + 3)
                    if g == 1:
                        unit_values_2()
                    rotate_piece(4 * g + 2)
                    rotate_piece(4 * g + 3)
                    if g == 0:
                        unit_values()
                    if g < 2:
                        weights_lo(2 * g + 4)
                a_lo(1)
                for u in range(UNITS + 2):
                    if u < UNITS:
                        maxima(u)
                    if 1 <= u <= UNITS:
                        pt_dve(u - 1)
                        row_recip(u - 1)
                    if u >= 2:
                        take_y(u - 2)
                    t, r = divmod(u - PAIRS, PAIRS)
                    if t >= 0 and r == 3 and u < UNITS:
                        dot(t)
                    if t >= 0 and r == 5 and u < UNITS:
                        take_along(t)
                dot(TB - 1)
                take_along(TB - 1)
                xt_lo(1)
                low_rank_lo(1)
                weights_lo(8)
                weights_lo(9)
                for o in range(12, 20):
                    t, c = o % 4, (o - 12) // 4
                    dve.wait_ge(s["out_ready"], o + 1)
                    dve.tensor_tensor(resid[:, t, c * W:(c + 1) * W], resid[:, t, c * W:(c + 1) * W],
                                      bank[:, 4 * ((o // 4) % 2) + t, :], ALU.add)




E, EG, GSZ = 16, 4, 4
F = 2048
MI = 512
TOPK = 2
MAXC = (TOPK * T - E) // P + E
NC = MAXC + 1
MINC = TOPK * T // P
AWAY = -1e30


def routed_and_shared(nc, m, ins, resid, ident, plan, xn_dram, y_dram, ln):
    slots_i, weights, tokens_i, meta = plan
    UP, PIECES = 8, 16
    names = """w_loaded0 w_loaded1 tab_loaded consts_done 
        xt_ready xt_hi_done xt_lo_done w_hi_done w_split w_used rw_hi_done rw_split logits_ready exp_done
        route mask_done pos_ready ab_done tok_ready out_ready relu_done a_done a_hi a_lo
        xn_stored zeros_done y_cleared""".split()
    s = {n: m.sem("d_" + n) for n in names}

    with ExitStack() as stage:
        sb = lambda *a: m.sb(*a, stack=stage)
        raw = sb("d_raw", [P, 2, 2048])
        w_hi, w_lo = sb("d_w_hi", [P, 2, 4, W], F32R), sb("d_w_lo", [P, 2, 4, W], F32R)
        xT_hi, xT_lo = sb("d_xT_hi", [P, DB, T], F32R), sb("d_xT_lo", [P, DB, T], F32R)
        aT_hi, aT_lo = sb("d_aT_hi", [P, F // P, T], F32R), sb("d_aT_lo", [P, F // P, T], F32R)
        xn = sb("d_xn", [P, TB, D])
        relu = lambda o: xn[:, o % 2, 0:W]
        square = lambda o: xn[:, o % 2, W:2 * W]
        zeros = sb("d_zeros", [P, D])
        rw = sb("d_rw", [P, DB, E])
        rw_hi, rw_lo = sb("d_rw_hi", [P, DB, E], F32R), sb("d_rw_lo", [P, DB, E], F32R)
        stats, mean_var = sb("d_stats", [P, TB, 2, 6]), sb("d_mean_var", [P, TB, 2])
        rstd, consts = sb("d_rstd", [P, TB]), sb("d_consts", [P, 2])
        ones, below = sb("d_ones", [P, P]), sb("d_below", [P, P])
        iota = sb("d_iota", [P, P])
        rank = sb("d_rank", [P, E])
        tok_id = sb("d_tok_id", [P, TB])
        e_bias = sb("d_e_bias", [P, E])
        big = lambda n: sb(n, [P, TB, E])
        score, biased, left, key, mask = (big("d_score"), big("d_biased"), big("d_left"), big("d_key"),
                                          big("d_mask"))
        pick = [big("d_pick0"), big("d_pick1")]
        small = lambda n: sb(n, [P, TB, EG])
        gmax, gscore, gleft, gkey, gpick, gmask = (small("d_gmax"), small("d_gscore"), small("d_gleft"),
                                                   small("d_gkey"), small("d_gpick"), small("d_gmask"))
        top = sb("d_top", [P, TB])
        wsum = sb("d_wsum", [P, TB])
        chunks, chunk_end, zero16 = sb("d_chunks", [P, E]), sb("d_chunk_end", [P, E]), sb("d_zero16", [P, E])
        first_slot = sb("d_first_slot", [P, E])
        pos = sb("d_pos", [P, TOPK, TB])
        slot = sb("d_slot", [P, TOPK, TB])
        chunk, lane = sb("d_chunk", [P, TOPK, TB]), sb("d_lane", [P, TOPK, TB])
        is_lane = sb("d_is_lane", [P, TOPK * TB, P])
        is_chunk = sb("d_is_chunk", [P, TOPK * TB, NC])
        ended = sb("d_ended", [P, NC, E])
        expert = sb("d_expert", [P, NC])
        bank = m.psum("d_banks", [P, 8, W], stack=stage)
        logits = bank[:, 5, 0:TB * E].rearrange("p (t e) -> p t e", e=E)
        before = bank[:, 5, 64:128].rearrange("p (t e) -> p t e", e=E)
        count = bank[:, 5, 128:144]
        tok_ps = bank[:, 5, 256:256 + NC]

        def piece_is_used(eng, w):
            if w < UP and w % 2:
                eng.wait_ge(s["out_ready"], 4 * (w // 2 + 1))
            elif w >= UP and w % 4 == 3:
                eng.wait_ge(s["out_ready"], 16 + 4 * ((w - UP) // 4 + 1))
            else:
                eng.wait_ge(s["w_used"], w // 2 + 1 if w < UP else 4 + 3 * ((w - UP) // 4) + w % 4 + 1)

        def xt_tile(x, n):
            t, h = divmod(n, 2)
            return x[:, 4 * h:4 * h + 4, t * P:(t + 1) * P]

        def xt_bank(n):
            return bank[:, 6 + n % 2, :].rearrange("p (e t) -> p e t", t=P)

        def out_bank(o):
            return bank[:, (0 if (o // 4) % 2 == 0 else 4) + o % 4, :]

        with nc.Block() as block:
            @block.sync
            def _(sp):
                for w in range(PIECES):
                    if w >= 2:
                        sp.wait_ge(s["w_split"], w - 1)
                    sp.dma_start(raw[:, w % 2, :], ins["shared_w"][w]).then_inc(s[f"w_loaded{w % 2}"], 16)
                    if w == 1:
                        sp.wait_ge(ln.xn_done, 3 * TB)
                        sp.dma_start(xn_dram.rearrange("(t p) d -> p t d", p=P),
                                     xn[:, :, :]).then_inc(s["xn_stored"], 16)
                    if w >= 4:
                        if w == 4:
                            sp.wait_ge(s["zeros_done"], 1)
                        for c in range(2 * (w - 4), min(2 * (w - 3), MAXC)):
                            sp.dma_start(y_dram[c * P:(c + 1) * P, :], zeros[:, :]).then_inc(s["y_cleared"], 16)
                sp.wait_ge(s["xn_stored"], 16)
                sp.wait_ge(s["y_cleared"], 16 * MAXC)

            @block.gpsimd
            def _(pool):
                loads = ((rw[:, :, :], ins["router_w"]), (tok_id[:, :], ins["tok_id"]),
                         (iota[:, :], ins["iota"].to_broadcast([P, P])),
                         (rank[:, :], ins["rank"].to_broadcast([P, E])),
                         (e_bias[:, :], ins["e_bias"].to_broadcast([P, E])))
                pool.memset(zeros[:, :], 0.0).then_inc(s["zeros_done"], 1)
                for out, in_ in loads:
                    pool.dma_start(out, in_).then_inc(s["tab_loaded"], 16)
                pool.memset(consts[:, 0:1], LN_EPS).then_inc(s["consts_done"], 1)
                pool.memset(consts[:, 1:2], -0.5).then_inc(s["consts_done"], 1)
                pool.memset(ones[:, :], 1.0).then_inc(s["consts_done"], 1)
                pool.memset(zero16[:, :], 0.0).then_inc(s["consts_done"], 1)
                pool.wait_ge(s["consts_done"], 4)
                for t in range(TB):
                    ln.rstd(pool, 2, mean_var, rstd, consts, t)
                pool.affine_select(out=below[:, :], in_=ones[:, :], compare_op=ALU.is_gt, fill=0.0,
                                   base=0, pattern=[[1, P]], channel_multiplier=-1).then_inc(s["consts_done"], 1)

            @block.tensor
            def _(pe):
                for n in range(2 * TB):
                    t, h = divmod(n, 2)
                    pe.wait_ge(ln.xn_done, 2 * TB + t + 1)
                    if n >= 2:
                        pe.wait_ge(s["xt_lo_done"], n - 1)
                    for i in range(4):
                        e = 4 * h + i
                        mm = pe.transpose(xt_bank(n)[:, i, :], xn[:, t, e * P:(e + 1) * P], ident[:, :])
                    mm.then_inc(s["xt_ready"], 1)
                pe.wait_ge(s["xt_lo_done"], 2 * TB)
                pe.wait_ge(s["rw_split"], 1)
                for t in range(TB):
                    for e in range(DB):
                        mm = matmul_3pass(logits[:, t, :], xT_hi[:, e, t * P:(t + 1) * P],
                                          xT_lo[:, e, t * P:(t + 1) * P], rw_hi[:, e, :], rw_lo[:, e, :],
                                          e == 0, e == DB - 1)(pe)
                mm.then_inc(s["logits_ready"], 1)

                def up(w):
                    g, h = divmod(w, 2)
                    pe.wait_ge(s["w_split"], w + 1)
                    for i in range(4):
                        o = 4 * g + i
                        if h == 0 and g >= 2:
                            pe.wait_ge(s["relu_done"], o - 7)
                        if h == 0 and g == 1 and i == 1:
                            pe.wait_ge(s["ab_done"], 2)
                        for j in range(4):
                            e = 4 * h + j
                            mm = matmul_3pass(out_bank(o), w_hi[:, w % 2, j, i * P:(i + 1) * P],
                                              w_lo[:, w % 2, j, i * P:(i + 1) * P],
                                              xT_hi[:, e, :], xT_lo[:, e, :], e == 0, e == DB - 1)(pe)
                        if h == 1:
                            mm.then_inc(s["out_ready"], 1)
                    if h == 0:
                        mm.then_inc(s["w_used"], 1)

                def down(w):
                    c, q = divmod(w - UP, 4)
                    pe.wait_ge(s["w_split"], w + 1)
                    for t in range(TB):
                        o = 16 + 4 * c + t
                        if q == 0:
                            pe.wait_ge(s["relu_done"], o - 7 if c == 0 else 16)
                            if c == 0 and t == 0:
                                pe.wait_ge(s["a_lo"], 16)
                        for j in range(4):
                            f = 4 * q + j
                            mm = matmul_3pass(out_bank(o), aT_hi[:, f, t * P:(t + 1) * P],
                                              aT_lo[:, f, t * P:(t + 1) * P], w_hi[:, w % 2, j, :],
                                              w_lo[:, w % 2, j, :], f == 0, f == F // P - 1)(pe)
                        if q == 3:
                            mm.then_inc(s["out_ready"], 1)
                    if q < 3:
                        mm.then_inc(s["w_used"], 1)

                up(0)
                pe.wait_ge(s["mask_done"], 1)
                pe.wait_ge(s["consts_done"], 5)
                for t in range(TB):
                    for b in range(t):
                        pe.matmul(before[:, t, :], ones[:, :], mask[:, b, :], start=b == 0, stop=False)
                    pe.matmul(before[:, t, :], below[:, :], mask[:, t, :], start=t == 0, stop=True)
                for b in range(TB):
                    mm = pe.matmul(count, ones[:, :], mask[:, b, :], start=b == 0, stop=b == TB - 1)
                mm.then_inc(s["pos_ready"], 1)
                up(1)
                pe.wait_ge(s["ab_done"], 1)
                for i in range(TOPK * TB):
                    mm = pe.matmul(tok_ps, is_lane[:, i, :], is_chunk[:, i, :], start=i == 0,
                                   stop=i == TOPK * TB - 1)
                mm.then_inc(s["tok_ready"], 1)
                for w in range(2, UP):
                    up(w)
                for w in range(UP, PIECES):
                    down(w)

            @block.scalar
            def _(act):
                def weights_hi(w):
                    act.wait_ge(s[f"w_loaded{w % 2}"], 16 * (w // 2 + 1))
                    if w >= 2:
                        piece_is_used(act, w - 2)
                    act.activation(w_hi[:, w % 2, :, :], raw[:, w % 2, :].rearrange("p (e n) -> p e n", n=W),
                                   ACT.Copy).then_inc(s["w_hi_done"], 1)

                weights_hi(0)
                weights_hi(1)
                act.wait_ge(s["tab_loaded"], 80)
                act.activation(rw_hi[:, :, :], rw[:, :, :], ACT.Copy).then_inc(s["rw_hi_done"], 1)
                for n in range(2 * TB):
                    act.wait_ge(s["xt_ready"], n + 1)
                    act.activation(xt_tile(xT_hi, n), xt_bank(n), ACT.Copy).then_inc(s["xt_hi_done"], 1)
                act.wait_ge(s["logits_ready"], 1)
                act.activation(score[:, :, :], logits, ACT.Exp, scale=-1.0).then_inc(s["exp_done"], 1)
                act.wait_ge(s["xn_stored"], 16)
                for g in range(4):
                    weights_hi(2 * g + 2)
                    for o in range(4 * g, 4 * g + 4):
                        act.wait_ge(s["out_ready"], o + 1)
                        if o >= 2:
                            act.wait_ge(s["a_done"], o - 1)
                        act.activation(relu(o), out_bank(o), ACT.Relu).then_inc(s["relu_done"], 1)
                        act.wait_ge(s["a_done"], o + 1)
                        act.activation(aT_hi[:, o, :], square(o), ACT.Copy).then_inc(s["a_hi"], 1)
                    weights_hi(2 * g + 3)
                for w in range(UP + 2, PIECES):
                    weights_hi(w)

            @block.vector
            def _(dve):
                def weights_lo(w):
                    dve.wait_ge(s["w_hi_done"], w + 1)
                    dve.tensor_tensor(w_lo[:, w % 2, :, :], raw[:, w % 2, :].rearrange("p (e n) -> p e n", n=W),
                                      f32(w_hi[:, w % 2, :, :]), ALU.subtract).then_inc(s["w_split"], 1)

                for t in range(TB):
                    ln.stats(dve, 2, resid, stats, mean_var, t)
                for t in range(TB):
                    ln.norm(dve, 2, resid, xn, mean_var, rstd, t)
                dve.wait_ge(s["rw_hi_done"], 1)
                dve.tensor_tensor(rw_lo[:, :, :], rw[:, :, :], f32(rw_hi[:, :, :]),
                                  ALU.subtract).then_inc(s["rw_split"], 1)
                for n in range(2 * TB):
                    dve.wait_ge(s["xt_hi_done"], n + 1)
                    dve.tensor_tensor(xt_tile(xT_lo, n), xt_bank(n), f32(xt_tile(xT_hi, n)),
                                      ALU.subtract).then_inc(s["xt_lo_done"], 1)
                weights_lo(0)
                weights_lo(1)

                def add_out(o):
                    t, c = o % 4, (o - 16) // 4
                    dve.wait_ge(s["out_ready"], o + 1)
                    dve.tensor_tensor(resid[:, t, c * W:(c + 1) * W], resid[:, t, c * W:(c + 1) * W],
                                      out_bank(o), ALU.add)

                steps = [0]

                def step(op):
                    steps[0] += 1
                    op.then_inc(s["route"], 1)
                    dve.wait_ge(s["route"], steps[0])

                def first_of_max(out, x, top, key, rank, shape):
                    whole = top.unsqueeze(2).to_broadcast(shape)
                    step(dve.tensor_reduce(top, x, AX.X, ALU.max))
                    step(dve.tensor_tensor(key, x, whole, ALU.is_equal))
                    step(dve.tensor_tensor(key, key, rank, ALU.mult))
                    step(dve.tensor_reduce(top, key, AX.X, ALU.max))
                    step(dve.tensor_tensor(out, key, whole, ALU.is_equal))

                dve.wait_ge(s["exp_done"], 1)
                step(dve.tensor_scalar(score[:, :, :], score[:, :, :], 1.0, None, ALU.add))
                step(dve.reciprocal(score[:, :, :], score[:, :, :]))
                step(dve.tensor_tensor(biased[:, :, :], score[:, :, :],
                                       e_bias[:, :].unsqueeze(1).to_broadcast([P, TB, E]), ALU.add))
                by_group = lambda x: x[:, :, :].rearrange("p t (g k) -> p (t g) k", k=GSZ)
                flat = lambda x: x[:, :, :].rearrange("p t g -> p (t g)")
                gshape = [P, TB * EG, GSZ]
                step(dve.tensor_reduce(flat(gscore), by_group(biased), AX.X, ALU.max))
                first_of_max(by_group(pick[0]), by_group(biased), flat(gmax), by_group(key),
                             rank[:, E - GSZ:E].unsqueeze(1).to_broadcast(gshape), gshape)
                step(dve.scalar_tensor_tensor(flat(left), flat(pick[0]), AWAY, flat(biased), ALU.mult, ALU.add))
                step(dve.tensor_reduce(flat(gmax), by_group(left), AX.X, ALU.max))
                step(dve.tensor_tensor(flat(gscore), flat(gscore), flat(gmax), ALU.add))
                sshape = [P, TB, EG]
                srank = rank[:, E - EG:E].unsqueeze(1).to_broadcast(sshape)
                first_of_max(gmask[:, :, :], gscore[:, :, :], top[:, :], gkey[:, :, :], srank, sshape)
                step(dve.scalar_tensor_tensor(flat(gleft), flat(gmask), AWAY, flat(gscore), ALU.mult, ALU.add))
                first_of_max(gpick[:, :, :], gleft[:, :, :], top[:, :], gkey[:, :, :], srank, sshape)
                step(dve.tensor_tensor(flat(gmask), flat(gmask), flat(gpick), ALU.add))
                step(dve.tensor_tensor(by_group(left), by_group(biased),
                                       flat(gmask).unsqueeze(2).to_broadcast(gshape), ALU.mult))
                eshape = [P, TB, E]
                erank = rank[:, :].unsqueeze(1).to_broadcast(eshape)
                first_of_max(pick[0][:, :, :], left[:, :, :], top[:, :], key[:, :, :], erank, eshape)
                step(dve.scalar_tensor_tensor(flat(left), flat(pick[0]), AWAY, flat(left), ALU.mult, ALU.add))
                first_of_max(pick[1][:, :, :], left[:, :, :], top[:, :], key[:, :, :], erank, eshape)
                dve.tensor_tensor(flat(mask), flat(pick[0]), flat(pick[1]), ALU.add).then_inc(s["mask_done"], 1)
                for k in range(TOPK):
                    step(dve.tensor_tensor(flat(key), flat(score), flat(pick[k]), ALU.mult))
                    step(dve.tensor_reduce(weights[:, k, :], key[:, :, :], AX.X, ALU.add))
                step(dve.tensor_tensor(wsum[:, :], weights[:, 0, :], weights[:, 1, :], ALU.add))
                step(dve.tensor_scalar(wsum[:, :], wsum[:, :], 1e-20, None, ALU.add))
                step(dve.reciprocal(wsum[:, :], wsum[:, :]))
                for k in range(TOPK):
                    step(dve.tensor_tensor(weights[:, k, :], weights[:, k, :], wsum[:, :], ALU.mult))
                dve.wait_ge(s["pos_ready"], 1)
                step(dve.tensor_scalar(chunks[:, :], count, 0.5, None, ALU.is_gt))
                for n in range(1, T // P):
                    step(dve.scalar_tensor_tensor(chunks[:, :], count, n * P + 0.5, chunks[:, :],
                                                  ALU.is_gt, ALU.add))
                step(dve.tensor_tensor_scan(chunk_end[:, :], chunks[:, :], zero16[:, :], 0.0, ALU.add, ALU.add))
                step(dve.tensor_tensor(first_slot[:, :], chunk_end[:, :], chunks[:, :], ALU.subtract))
                for k in range(TOPK):
                    step(dve.tensor_tensor(key[:, :, :], before, pick[k][:, :, :], ALU.mult))
                    step(dve.tensor_reduce(pos[:, k, :], key[:, :, :], AX.X, ALU.add))
                    step(dve.tensor_tensor(key[:, :, :], pick[k][:, :, :],
                                           first_slot[:, :].unsqueeze(1).to_broadcast(eshape), ALU.mult))
                    step(dve.tensor_reduce(chunk[:, k, :], key[:, :, :], AX.X, ALU.add))
                kt = lambda x: x[:, :, :].rearrange("p k t -> p (k t)")
                step(dve.scalar_tensor_tensor(kt(slot), kt(chunk), float(P), kt(pos), ALU.mult, ALU.add))
                step(dve.tensor_copy(slots_i[:, :, :], slot[:, :, :]))
                for n in range(1, T // P):
                    step(dve.scalar_tensor_tensor(kt(chunk), kt(pos), n * P - 0.5, kt(chunk), ALU.is_gt, ALU.add))
                step(dve.scalar_tensor_tensor(kt(lane), kt(chunk), -float(P), kt(slot), ALU.mult, ALU.add))
                for i in range(TOPK * TB):
                    k, t = divmod(i, TB)
                    dve.tensor_scalar(is_lane[:, i, :], iota[:, :], lane[:, k, t:t + 1], None, ALU.is_equal)
                    ab = dve.tensor_scalar(is_chunk[:, i, :], iota[:, 0:NC], chunk[:, k, t:t + 1],
                                           tok_id[:, t:t + 1], ALU.is_equal, ALU.mult)
                ab.then_inc(s["ab_done"], 1)
                step(dve.tensor_tensor(ended[:, :, :], chunk_end[:, :].unsqueeze(1).to_broadcast([P, NC, E]),
                                       iota[:, 0:NC].unsqueeze(2).to_broadcast([P, NC, E]), ALU.is_le))
                step(dve.tensor_reduce(expert[:, :], ended[:, :, :], AX.X, ALU.add))
                step(dve.tensor_scalar(expert[:, :], expert[:, :], float(E - 1), None, ALU.min))
                step(dve.tensor_copy(meta[:, 0:NC, 0], expert[:, :]))
                step(dve.tensor_scalar(meta[:, NC:NC + 1, 0], chunk_end[:, E - 1:E], -1.0, None, ALU.add))
                dve.wait_ge(s["tok_ready"], 1)
                dve.tensor_copy(tokens_i[:, :, 0], tok_ps).then_inc(s["ab_done"], 1)

                for g in range(4):
                    weights_lo(2 * g + 2)
                    for o in range(4 * g, 4 * g + 4):
                        dve.wait_ge(s["relu_done"], o + 1)
                        if o >= 2:
                            dve.wait_ge(s["a_lo"], o - 1)
                        dve.tensor_tensor(square(o), relu(o), relu(o), ALU.mult).then_inc(s["a_done"], 1)
                        dve.wait_ge(s["a_hi"], o + 1)
                        dve.tensor_tensor(aT_lo[:, o, :], square(o), f32(aT_hi[:, o, :]),
                                          ALU.subtract).then_inc(s["a_lo"], 1)
                    weights_lo(2 * g + 3)
                for w in range(UP + 2, PIECES):
                    weights_lo(w)
                    if w == PIECES - 2:
                        for o in range(16, 20):
                            add_out(o)
                for o in range(20, 24):
                    add_out(o)


def experts(nc, m, ins, resid, ident, plan, xn_dram, y_dram, out):
    slots_i, weights, tokens_i, meta = plan
    names = """up_loaded down_loaded idx_done idx_seen sp_waited gathered t1_ready t1_act t1_dve up_ready relu_done a_done t2_ready
        t2_act t2_dve down_ready y_act y_dve y_stored row_free rows0 rows1 rows2 rows3 add_done out_stored""".split()
    s = {n: m.sem("e_" + n) for n in names}
    with ExitStack() as stage:
        sb = lambda *a: m.sb(*a, stack=stage)
        w_up = sb("e_w_up", [P, 2, DB, MI])
        w_down = sb("e_w_down", [P, 2, MI // P, D])
        idx = sb("e_idx", [P, 1], I32)
        xg = sb("e_xg", [P, D])
        xgT = sb("e_xgT", [P, DB, P])
        r_sb, a_sb = sb("e_relu", [P, MI]), sb("e_a", [P, MI])
        aT = sb("e_aT", [P, MI // P, P])
        y_sb = sb("e_y", [P, D])
        rows = sb("e_rows", [P, 4, D])
        bank = m.psum("e_banks", [P, 8, W], stack=stage)
        blocks = lambda ap: ap.rearrange("p (e t) -> p e t", t=P)

        def last_chunk(eng):
            return eng.value_load(meta[0:1, NC, 0:1], min_val=MINC - 1, max_val=MAXC - 1)

        with nc.Block() as block:
            @block.sync
            def _(sp):
                last = last_chunk(sp)

                def load(c, known):
                    e = sp.value_load(meta[0:1, c, 0:1], min_val=0, max_val=E - 1)
                    par = c % 2
                    if known >= 1:
                        sp.wait_ge(s["up_loaded"], c * 16)
                        sp.sem_inc(s["sp_waited"], 1)
                    if known >= 2:
                        sp.wait_ge(s["up_ready"], c - 1)
                        sp.sem_inc(s["sp_waited"], 1)
                    sp.dma_start(w_up[:, par, :, :], ins["w_up"][e]).then_inc(s["up_loaded"], 16)
                    if known >= 1:
                        sp.wait_ge(s["down_loaded"], c * 16)
                        sp.sem_inc(s["sp_waited"], 1)
                    if known >= 2:
                        sp.wait_ge(s["down_ready"], c - 1)
                        sp.sem_inc(s["sp_waited"], 1)
                    sp.dma_start(w_down[:, par, :, :], ins["w_down"][e]).then_inc(s["down_loaded"], 16)

                load(0, 0)
                load(1, 1)
                with sp.Fori(2, last + 1) as c:
                    load(c, 2)

            @block.gpsimd
            def _(pool):
                last = last_chunk(pool)

                def gather(c, known):
                    if known:
                        pool.wait_ge(s["gathered"], c * 16)
                        pool.wait_ge(s["t1_ready"], c)
                    pool.tensor_copy(idx[:, :], tokens_i[:, c, :]).then_inc(s["idx_done"], 1)
                    pool.wait_ge(s["idx_done"], c + 1)
                    pool.sem_inc(s["idx_seen"], 1)
                    pool.indirect_dma_start(xg[:, :], None, xn_dram, bass.IndirectOffsetOnAxis(ap=idx[:, :], axis=0),
                                            ).then_inc(s["gathered"], 16)

                gather(0, 0)
                with pool.Fori(1, last + 2) as c:
                    gather(c, 1)
                pool.wait_ge(s["y_stored"], (last + 1) * 16)
                pool.sem_inc(s["idx_seen"], 1)
                for i in range(TOPK * TB):
                    t, k = divmod(i, TOPK)
                    if i >= 4:
                        pool.wait_ge(s["add_done"], i - 3)
                    pool.indirect_dma_start(rows[:, i % 4, :], None, y_dram,
                                            bass.IndirectOffsetOnAxis(ap=slots_i[:, k, t:t + 1], axis=0),
                                            ).then_inc(s[f"rows{i % 4}"], 16)

            @block.tensor
            def _(pe):
                last = last_chunk(pe)

                def turn_tokens(c, known):
                    pe.wait_ge(s["gathered"], (c + 1) * 16)
                    if known:
                        pe.wait_ge(s["t1_act"], c)
                        pe.wait_ge(s["t1_dve"], c)
                    for e in range(DB):
                        mm = pe.transpose(bank[:, e // 4, (e % 4) * P:(e % 4 + 1) * P],
                                          xg[:, e * P:(e + 1) * P], ident[:, :])
                    mm.then_inc(s["t1_ready"], 1)

                def up(c, known):
                    pe.wait_ge(s["t1_act"], c + 1)
                    pe.wait_ge(s["t1_dve"], c + 1)
                    pe.wait_ge(s["up_loaded"], (c + 1) * 16)
                    if known:
                        pe.wait_ge(s["relu_done"], c)
                    for e in range(DB):
                        mm = pe.matmul(bank[:, 2, :], xgT[:, e, :], w_up[:, c % 2, e, :], start=e == 0,
                                       stop=e == DB - 1)
                    mm.then_inc(s["up_ready"], 1)

                def down(c, known):
                    pe.wait_ge(s["a_done"], c + 1)
                    if known:
                        pe.wait_ge(s["t2_act"], c)
                    for f in range(MI // P):
                        mm = pe.transpose(bank[:, 3, f * P:(f + 1) * P], a_sb[:, f * P:(f + 1) * P], ident[:, :])
                    mm.then_inc(s["t2_ready"], 1)
                    pe.wait_ge(s["t2_act"], c + 1)
                    pe.wait_ge(s["down_loaded"], (c + 1) * 16)
                    if known:
                        pe.wait_ge(s["y_act"], c)
                        pe.wait_ge(s["y_dve"], c)
                    for h in range(2):
                        for f in range(MI // P):
                            mm = pe.matmul(bank[:, 4 + h, :], aT[:, f, :], w_down[:, c % 2, f, h * W:(h + 1) * W],
                                           start=f == 0, stop=f == MI // P - 1)
                    mm.then_inc(s["down_ready"], 1)

                turn_tokens(0, 0)
                up(0, 0)
                turn_tokens(1, 1)
                up(1, 1)
                turn_tokens(2, 1)
                down(0, 0)
                with pe.Fori(1, last) as c:
                    up(c + 1, 1)
                    turn_tokens(c + 2, 1)
                    down(c, 1)
                down(last, 1)

            @block.scalar
            def _(act):
                last = last_chunk(act)

                def t1(c, known):
                    act.wait_ge(s["t1_ready"], c + 1)
                    if known:
                        act.wait_ge(s["up_ready"], c)
                    act.activation(xgT[:, 0:4, :], blocks(bank[:, 0, :]), ACT.Copy).then_inc(s["t1_act"], 1)

                def relu(c, known):
                    act.wait_ge(s["up_ready"], c + 1)
                    if known:
                        act.wait_ge(s["a_done"], c)
                    act.activation(r_sb[:, :], bank[:, 2, :], ACT.Relu).then_inc(s["relu_done"], 1)

                def t2_y(c, known):
                    act.wait_ge(s["t2_ready"], c + 1)
                    if known:
                        act.wait_ge(s["down_ready"], c)
                    act.activation(aT[:, :, :], blocks(bank[:, 3, :]), ACT.Copy).then_inc(s["t2_act"], 1)
                    act.wait_ge(s["down_ready"], c + 1)
                    if known:
                        act.wait_ge(s["y_stored"], c * 16)
                    act.activation(y_sb[:, 0:W], bank[:, 4, :], ACT.Copy).then_inc(s["y_act"], 1)
                    act.wait_ge(s["y_act"], c + 1)
                    act.wait_ge(s["y_dve"], c + 1)
                    act.dma_start(y_dram.rearrange("(c p) d -> c p d", p=P)[c], y_sb[:, :]).then_inc(s["y_stored"], 16)

                t1(0, 0)
                relu(0, 0)
                t1(1, 1)
                relu(1, 1)
                t1(2, 1)
                t2_y(0, 0)
                with act.Fori(1, last) as c:
                    relu(c + 1, 1)
                    t1(c + 2, 1)
                    t2_y(c, 1)
                t2_y(last, 1)
                for t in range(TB):
                    act.wait_ge(s["add_done"], 2 * t + 2)
                    act.dma_start(out[t], resid[:, t, :]).then_inc(s["out_stored"], 16)
                act.wait_ge(s["out_stored"], 16 * TB)

            @block.vector
            def _(dve):
                last = last_chunk(dve)

                def t1(c, known):
                    dve.wait_ge(s["t1_ready"], c + 1)
                    if known:
                        dve.wait_ge(s["up_ready"], c)
                    dve.tensor_copy(xgT[:, 4:8, :], blocks(bank[:, 1, :])).then_inc(s["t1_dve"], 1)

                def square(c, known):
                    dve.wait_ge(s["relu_done"], c + 1)
                    if known:
                        dve.wait_ge(s["t2_ready"], c)
                    dve.tensor_tensor(a_sb[:, :], r_sb[:, :], r_sb[:, :], ALU.mult).then_inc(s["a_done"], 1)

                def y_half(c, known):
                    dve.wait_ge(s["down_ready"], c + 1)
                    if known:
                        dve.wait_ge(s["y_stored"], c * 16)
                    dve.tensor_copy(y_sb[:, W:2 * W], bank[:, 5, :]).then_inc(s["y_dve"], 1)

                t1(0, 0)
                square(0, 0)
                t1(1, 1)
                t1(2, 1)
                square(1, 1)
                y_half(0, 0)
                with dve.Fori(1, last) as c:
                    t1(c + 2, 1)
                    square(c + 1, 1)
                    y_half(c, 1)
                y_half(last, 1)
                for i in range(TOPK * TB):
                    t, k = divmod(i, TOPK)
                    dve.wait_ge(s[f"rows{i % 4}"], 16 * (i // 4 + 1))
                    if k:
                        dve.wait_ge(s["add_done"], i)
                    dve.scalar_tensor_tensor(resid[:, t, :], rows[:, i % 4, :], weights[:, k, t:t + 1],
                                             resid[:, t, :], ALU.mult, ALU.add).then_inc(s["add_done"], 1)



def build(nc, ins, out):
    xn_dram = nc.dram_tensor("xn_dram", (T, D), F32, kind="Internal").ap()
    y_dram = nc.dram_tensor("y_dram", (MAXC * P, D), F32, kind="Internal").ap()
    with ExitStack() as stack:
        m = Memory(nc, stack)
        resid = m.sb("resid", [P, TB, D])
        ident = m.sb("ident", [P, P])
        ln = LayerNorm(m)
        with ExitStack() as stage:
            sb = lambda *a: m.sb(*a, stack=stage)
            QT = [sb(n, [P, DB, T], F32R) for n in ("QT_hi", "QT_lo")]
            K = [sb(n, [P, 2, DB, W], F32R) for n in ("K_hi", "K_lo")]
            V = [sb(n, [P, 2, 4, D], F32R) for n in ("V_hi", "V_lo")]
            raw = sb("raw", [P, 2, 2048])
            kv_loaded = [m.sem(f"kv_loaded{i}") for i in range(2)]
            cross_projections(nc, m, ins, resid, QT, K, V, raw, kv_loaded, ident, ln)
            cross_attention(nc, m, ins, resid, QT, K, V, raw, kv_loaded, ident)
        self_attention(nc, m, ins, resid, ident, ln)
        plan = (m.sb("slots_i", [P, TOPK, TB], I32), m.sb("weights", [P, TOPK, TB]),
                m.sb("tokens_i", [P, NC, 1], I32), m.sb("meta", [P, NC + 1, 1], I32))
        routed_and_shared(nc, m, ins, resid, ident, plan, xn_dram, y_dram, ln)
        experts(nc, m, ins, resid, ident, plan, xn_dram, y_dram, out)


def lay_out(a):
    f = np.float32
    c = np.ascontiguousarray
    col = lambda v: v.reshape(DB, P).T
    pieces = lambda w, cols: w.reshape(-1, 4, P, cols, W).transpose(3, 0, 2, 1, 4).reshape(-1, P, 4 * W)
    x, ctx = a["x"][0], a["ctx_2048"][0]
    past = ctx[:ctx.shape[0] - T]
    k = past.reshape(-1, T, 2, 4, P).transpose(0, 2, 4, 3, 1).reshape(-1, 2, P, 4 * W)
    v = past.reshape(-1, 2, 2, P, D).transpose(0, 1, 3, 2, 4).reshape(-1, 2, P, 2 * D)
    mask = a["mask_BxSxS2_ff0"][0].reshape(TB, P, -1, W).transpose(2, 0, 1, 3)
    att = lambda n: a["L0_attn_" + n]
    ffn = lambda n: a["L0_ffn_" + n]
    A = np.zeros((2, D, P), f)
    A[0, :, 0:16], A[0, :, 16:32], A[0, :, 32:48], A[1, :, 0:16] = att("q_A"), att("k_A"), att("v_A"), att("p_A")
    B = np.zeros((P, 5 * W), f)
    B[16:32, 0:256], B[32:48, 256:512], B[0:16, 512:1536], B[0:16, 1536:] = (
        att("k_B"), att("v_B"), att("q_B"), att("p_B"))
    inv_freq = f(1.0) / f(10000.0) ** (np.arange(0, HD, 2, dtype=f) / f(HD))
    angle = (np.arange(T, dtype=f)[:, None] * inv_freq[None, :]).astype(np.float64)
    table = lambda t: c(t.astype(f).reshape(TB, P, HD // 2).transpose(1, 0, 2))
    return {
        "x": c(x.reshape(TB, P, D)),
        "xattn_w": c(np.concatenate([pieces(a["L0_xattn_W" + n].T, 2) for n in "qkv"])),
        "xattn_b_cols": c(np.concatenate([col(a["L0_xattn_bq"]), col(a["L0_xattn_bk"])], 1)),
        "xattn_bv": c(a["L0_xattn_bv"].reshape(1, D)),
        "kv": c(np.concatenate([k, v], 1).reshape(-1, P, 2048)),
        "mask": c(np.concatenate([mask[-1:], mask[:-1]]).reshape(-1, P, W)),
        "attn_w": c(pieces(np.concatenate([att("Wk"), att("Wv"), att("Wq"), att("Wproj")], 1), 5)),
        "attn_A": c(A.reshape(2, DB, P, P).transpose(0, 2, 1, 3)),
        "attn_B": c(B.reshape(P, 5, W)),
        "cos": table(np.cos(angle)),
        "sin": table(np.sin(angle)),
        "gain": c(att("q_gain").reshape(1, H)),
        "shared_w": c(np.concatenate([pieces(ffn("shared_up"), 4), pieces(ffn("shared_down"), 2)])),
        "router_w": c(ffn("router_weight").T.reshape(DB, P, E).transpose(1, 0, 2)),
        "e_bias": c(ffn("e_bias").reshape(1, E)),
        "iota": np.arange(P, dtype=f).reshape(1, P),
        "rank": np.arange(E, 0, -1, dtype=f).reshape(1, E),
        "tok_id": c(np.arange(T, dtype=f).reshape(TB, P).T),
        "w_up": c(ffn("w_up").reshape(E, DB, P, MI).transpose(0, 2, 1, 3)),
        "w_down": c(ffn("w_down").reshape(E, MI // P, P, D).transpose(0, 2, 1, 3)),
    }


def kernel(**inputs):
    import concourse.bacc as bacc
    from concourse.bass_utils import run_bass_kernel_spmd

    arrays = lay_out({n: np.asarray(v) for n, v in inputs.items()})
    nc = bacc.Bacc("TRN2", target_bir_lowering=False, num_devices=1, dynamic_dma_scratch_size=8192)
    ins = {n: nc.dram_tensor(n, v.shape, mybir.dt.from_np(v.dtype), kind="ExternalInput").ap()
           for n, v in arrays.items()}
    out = nc.dram_tensor("out", (TB, P, D), F32, kind="ExternalOutput").ap()
    build(nc, ins, out)
    result = run_bass_kernel_spmd(nc, [arrays], core_ids=[0]).results[0]["out"]
    return result.reshape(1, T, D)
```
